# Optimizing a Trainium2 kernel written in Bass

```python
import numpy as np
import jax
import jax.numpy as jnp

def _softmax(x, axis=-1):
    return jax.nn.softmax(x, axis=axis)

def _gelu(x):
    return jax.nn.gelu(x, approximate=True)

def _silu(x):
    return jax.nn.silu(x)

def _sigmoid(x):
    return jax.nn.sigmoid(x)

def _layernorm(x, axis=-1, eps=1e-05):
    m = jnp.mean(x, axis=axis, keepdims=True)
    v = jnp.var(x, axis=axis, keepdims=True)
    return (x - m) / jnp.sqrt(v + eps)

def _scatter_add(tgt, idx, src, axis=0):
    return tgt.at[idx].add(src)

def _segment_sum(src, seg, n):
    return jax.ops.segment_sum(src, seg, n)
kernel_name = 'mk_xattn_ffn_d1_seqx_r8_0b4619'

def setup_inputs(seed: int=0):
    np.random.seed(seed)
    _w = jnp.asarray

    def _rec_inputs():
        import jax
        import jax.numpy as jnp
        _rk = jax.random.key(seed)
        x = 7.22e-05 + 1 * jax.random.normal(jax.random.fold_in(_rk, 1), (16, 128, 128), jnp.float32)
        _lenS = 128 - jax.random.randint(jax.random.fold_in(_rk, 7), (16,), 0, max(1, 128 // 4) + 1, jnp.int32)
        _lenS2 = 128 - jax.random.randint(jax.random.fold_in(_rk, 8), (16,), 0, max(1, 128 // 4) + 1, jnp.int32)
        _ctx_1024P = jax.random.normal(jax.random.fold_in(_rk, 11), (16, 16, 128), jnp.float32)
        _ctx_1024c = jax.random.dirichlet(jax.random.fold_in(_rk, 511), 0.3 * jnp.ones((16,), jnp.float32), (16, 128))
        _ctx_1024t = jnp.einsum('bsk,bkd->bsd', _ctx_1024c, _ctx_1024P)
        _ctx_1024t = _ctx_1024t * jax.lax.rsqrt(jnp.mean(jnp.square(_ctx_1024t)) + 1e-12) * 0.953939
        ctx_1024 = 4.13588e-05 + 0.999923 * (_ctx_1024t + 0.3 * jax.random.normal(jax.random.fold_in(_rk, 611), (16, 128, 128), jnp.float32))
        return (x, ctx_1024)
    x, ctx_1024 = _rec_inputs()

    def _L0_xattn_setup():
        import jax, jax.numpy as jnp
        import numpy as np
        DIM = 128
        HEADS = 16
        DIM_HEAD = 64
        INNER = HEADS * DIM_HEAD
        CTX_DIM = 128
        key = jax.random.key(seed)
        ks = jax.random.split(key, 7)
        b, n, m = (4, 256, 256)
        x = jax.random.normal(ks[0], (b, n, DIM), dtype=jnp.float32)
        context = jax.random.normal(ks[1], (b, m, CTX_DIM), dtype=jnp.float32)
        s = 0.02
        W_q = jax.random.normal(ks[2], (DIM, INNER), dtype=jnp.float32) * s
        W_k = jax.random.normal(ks[3], (CTX_DIM, INNER), dtype=jnp.float32) * s
        W_v = jax.random.normal(ks[4], (CTX_DIM, INNER), dtype=jnp.float32) * s
        W_o = jax.random.normal(ks[5], (INNER, DIM), dtype=jnp.float32) * s
        b_o = jax.random.normal(ks[6], (DIM,), dtype=jnp.float32) * s
        return {'x': x, 'context': context, 'W_q': W_q, 'W_k': W_k, 'W_v': W_v, 'W_o': W_o, 'b_o': b_o}
    _L0_xattn_all = _L0_xattn_setup()
    _L0_xattn_in = {k: v for k, v in _L0_xattn_all.items() if k in ('W_q', 'W_k', 'W_v', 'W_o', 'b_o')}
    del _L0_xattn_all

    def _L0_ffn_setup():
        import jax, jax.numpy as jnp
        import numpy as np
        B, S, H = (2, 256, 128)
        E_DYN, E_FIX = (8, 1)
        I_DYN, I_FIX = (64, 256)
        TOP_K = 4
        TOP_P = 0.75
        JITTER_EPS = 0.1
        CAPACITY_FACTOR = 1.25
        MIN_CAPACITY = 4

        def _sparse_mixer(scores):
            T = scores.shape[0]
            rows = jnp.arange(T)
            masked_scores = scores
            mults, sels = ([], [])
            for _ in range(TOP_K):
                thr = jnp.max(masked_scores, axis=-1, keepdims=True)
                sel = jnp.argmax(masked_scores, axis=-1)
                factor = jnp.maximum(jnp.abs(scores), jnp.abs(thr))
                jmask = (thr - scores) / factor > 2.0 * JITTER_EPS
                gates = jax.nn.softmax(jnp.where(jmask, -jnp.inf, masked_scores), axis=-1)
                mult = jnp.take_along_axis(gates, sel[:, None], axis=-1)[:, 0]
                masked_scores = masked_scores.at[rows, sel].set(-jnp.inf)
                mults.append(mult)
                sels.append(sel)
            return (jnp.stack(mults, axis=-1), jnp.stack(sels, axis=-1))
        key = jax.random.key(seed)
        k = jax.random.split(key, 8)
        sc = 0.02
        return {'hidden_states': jax.random.normal(k[0], (B, S, H), jnp.float32), 'gate_w': jax.random.normal(k[1], (E_DYN + E_FIX, H), jnp.float32) * sc, 'dyn_gate_w': jax.random.normal(k[2], (E_DYN, I_DYN, H), jnp.float32) * sc, 'dyn_up_w': jax.random.normal(k[3], (E_DYN, I_DYN, H), jnp.float32) * sc, 'dyn_down_w': jax.random.normal(k[4], (E_DYN, H, I_DYN), jnp.float32) * sc, 'sh_gate_w': jax.random.normal(k[5], (E_FIX, I_FIX, H), jnp.float32) * sc, 'sh_up_w': jax.random.normal(k[6], (E_FIX, I_FIX, H), jnp.float32) * sc, 'sh_down_w': jax.random.normal(k[7], (E_FIX, H, I_FIX), jnp.float32) * sc}
    _L0_ffn_all = _L0_ffn_setup()
    _L0_ffn_in = {k: v for k, v in _L0_ffn_all.items() if k in ('gate_w', 'dyn_gate_w', 'dyn_up_w', 'dyn_down_w', 'sh_gate_w', 'sh_up_w', 'sh_down_w')}
    del _L0_ffn_all
    return {'x': x, 'ctx_1024': ctx_1024, 'L0_xattn_W_q': _L0_xattn_in['W_q'], 'L0_xattn_W_k': _L0_xattn_in['W_k'], 'L0_xattn_W_v': _L0_xattn_in['W_v'], 'L0_xattn_W_o': _L0_xattn_in['W_o'], 'L0_xattn_b_o': _L0_xattn_in['b_o'], 'L0_ffn_gate_w': _L0_ffn_in['gate_w'], 'L0_ffn_dyn_gate_w': _L0_ffn_in['dyn_gate_w'], 'L0_ffn_dyn_up_w': _L0_ffn_in['dyn_up_w'], 'L0_ffn_dyn_down_w': _L0_ffn_in['dyn_down_w'], 'L0_ffn_sh_gate_w': _L0_ffn_in['sh_gate_w'], 'L0_ffn_sh_up_w': _L0_ffn_in['sh_up_w'], 'L0_ffn_sh_down_w': _L0_ffn_in['sh_down_w']}

def reference(x, ctx_1024, L0_xattn_W_q, L0_xattn_W_k, L0_xattn_W_v, L0_xattn_W_o, L0_xattn_b_o, L0_ffn_gate_w, L0_ffn_dyn_gate_w, L0_ffn_dyn_up_w, L0_ffn_dyn_down_w, L0_ffn_sh_gate_w, L0_ffn_sh_up_w, L0_ffn_sh_down_w):
    import jax
    import jax.numpy as jnp

    def _L0_xattn_ref(x, context, W_q, W_k, W_v, W_o, b_o):
        import jax, jax.numpy as jnp
        import numpy as np
        DIM = 128
        HEADS = 16
        DIM_HEAD = 64
        INNER = HEADS * DIM_HEAD
        CTX_DIM = 128
        b, n, _ = x.shape
        m = context.shape[1]
        h, d = (HEADS, DIM_HEAD)
        q = (x @ W_q).reshape(b, n, h, d).transpose(0, 2, 1, 3)
        k = (context @ W_k).reshape(b, m, h, d).transpose(0, 2, 1, 3)
        v = (context @ W_v).reshape(b, m, h, d).transpose(0, 2, 1, 3)
        sim = jnp.einsum('bhnd,bhmd->bhnm', q, k) * d ** (-0.5)
        attn = jax.nn.softmax(sim, axis=-1)
        out = jnp.einsum('bhnm,bhmd->bhnd', attn, v)
        out = out.transpose(0, 2, 1, 3).reshape(b, n, h * d)
        return out @ W_o + b_o

    def _L0_ffn_ref(hidden_states, gate_w, dyn_gate_w, dyn_up_w, dyn_down_w, sh_gate_w, sh_up_w, sh_down_w):
        import jax, jax.numpy as jnp
        import numpy as np
        B, S, H = (2, 256, 128)
        E_DYN, E_FIX = (8, 1)
        I_DYN, I_FIX = (64, 256)
        TOP_K = 4
        TOP_P = 0.75
        JITTER_EPS = 0.1
        CAPACITY_FACTOR = 1.25
        MIN_CAPACITY = 4

        def _sparse_mixer(scores):
            T = scores.shape[0]
            rows = jnp.arange(T)
            masked_scores = scores
            mults, sels = ([], [])
            for _ in range(TOP_K):
                thr = jnp.max(masked_scores, axis=-1, keepdims=True)
                sel = jnp.argmax(masked_scores, axis=-1)
                factor = jnp.maximum(jnp.abs(scores), jnp.abs(thr))
                jmask = (thr - scores) / factor > 2.0 * JITTER_EPS
                gates = jax.nn.softmax(jnp.where(jmask, -jnp.inf, masked_scores), axis=-1)
                mult = jnp.take_along_axis(gates, sel[:, None], axis=-1)[:, 0]
                masked_scores = masked_scores.at[rows, sel].set(-jnp.inf)
                mults.append(mult)
                sels.append(sel)
            return (jnp.stack(mults, axis=-1), jnp.stack(sels, axis=-1))
        Bv, Sv, Hv = hidden_states.shape
        T = Bv * Sv
        x = hidden_states.reshape(T, Hv)
        full_logits = x @ gate_w.T
        dyn_logits = full_logits[:, :E_DYN]
        probs = jax.nn.softmax(dyn_logits, axis=-1)
        sorted_p = jnp.sort(probs, axis=-1)[:, ::-1]
        csum = jnp.cumsum(sorted_p, axis=-1)
        dyn_k = jnp.minimum(jnp.sum(csum < TOP_P, axis=-1) + 1, TOP_K)
        mult, sel = _sparse_mixer(dyn_logits)
        slot_valid = jnp.arange(TOP_K)[None, :] < dyn_k[:, None]
        mult = jnp.where(slot_valid, mult, 0.0)
        rows = jnp.arange(T)
        rw = jnp.zeros((T, E_DYN), x.dtype).at[rows[:, None], sel].add(mult)
        rw = rw / jnp.sum(rw, axis=-1, keepdims=True)
        mask_dyn = (rw > 0).astype(jnp.int32)
        cap = max(int(np.ceil(T / E_DYN * CAPACITY_FACTOR)), MIN_CAPACITY)
        mask_dyn = mask_dyn * (jnp.cumsum(mask_dyn, axis=0) <= cap)
        expert_mask = jnp.concatenate([mask_dyn, jnp.ones((T, E_FIX), jnp.int32)], axis=-1)
        maskf = expert_mask.astype(x.dtype)
        gw = jax.nn.softmax(jnp.where(expert_mask == 0, -jnp.inf, full_logits), axis=-1)
        gd = rw * jnp.sum(gw[:, :E_DYN], axis=-1, keepdims=True)
        global_w = jnp.concatenate([gd, gw[:, E_DYN:]], axis=-1) * maskf
        g = jnp.einsum('th,eih->tei', x, dyn_gate_w)
        u = jnp.einsum('th,eih->tei', x, dyn_up_w)
        y_dyn = jnp.einsum('tei,ehi->teh', jax.nn.silu(g) * u, dyn_down_w)
        out = jnp.einsum('te,teh->th', global_w[:, :E_DYN], y_dyn)
        gs = jnp.einsum('th,fih->tfi', x, sh_gate_w)
        us = jnp.einsum('th,fih->tfi', x, sh_up_w)
        y_sh = jnp.einsum('tfi,fhi->tfh', jax.nn.silu(gs) * us, sh_down_w)
        out = out + jnp.einsum('tf,tfh->th', global_w[:, E_DYN:], y_sh)
        return out.reshape(Bv, Sv, Hv)
    x = x + _L0_xattn_ref(_layernorm(x, axis=-1), ctx_1024, L0_xattn_W_q, L0_xattn_W_k, L0_xattn_W_v, L0_xattn_W_o, L0_xattn_b_o)
    x = x + _L0_ffn_ref(_layernorm(x, axis=-1), L0_ffn_gate_w, L0_ffn_dyn_gate_w, L0_ffn_dyn_up_w, L0_ffn_dyn_down_w, L0_ffn_sh_gate_w, L0_ffn_sh_up_w, L0_ffn_sh_down_w)
    return x

_drawn_inputs = setup_inputs


def setup_inputs(seed=0):
    import zlib

    import numpy as np

    out = dict(_drawn_inputs(seed))
    spreads = {}
    factors = {'L0_xattn_W_q': 8.0,
     'L0_xattn_W_k': 8.0,
     'L0_ffn_gate_w': 8.0,
     'L0_ffn_dyn_gate_w': 8.0,
     'L0_ffn_dyn_up_w': 8.0,
     'L0_ffn_dyn_down_w': 8.0,
     'L0_ffn_sh_gate_w': 8.0,
     'L0_ffn_sh_up_w': 8.0,
     'L0_ffn_sh_down_w': 8.0}
    for name, (base, spread) in spreads.items():
        noise = np.random.default_rng([zlib.crc32(name.encode()), seed]).standard_normal(out[name].shape)
        drawn = base * np.exp(spread * noise) if base else spread * noise
        out[name] = jnp.asarray(drawn.astype(out[name].dtype))
    for name, factor in factors.items():
        out[name] = (out[name] * factor).astype(out[name].dtype)
    return out
```

```python
from contextlib import ExitStack

import concourse.bass as bass
from concourse import mybir

F32 = mybir.dt.float32
F32R = mybir.dt.float32r
BF16 = mybir.dt.bfloat16
ALU = mybir.AluOpType
ACT = mybir.ActivationFunctionType
X = mybir.AxisListType.X

P = 128
DH = 64
TOP_K = 4
TOP_P = 0.75
JITTER = 0.2
EPS = 1e-5
HIDE = 1e30



def xattn_moe(nc, x, ctx_t, wq_t, wk_t, w_v, w_o, b_o, gate_t, wg_t, wu_t, wd_t, out):
    B = x.shape[0]
    T = B * P
    H = wq_t.shape[1] // P
    PAIRS = B // 2
    GROUPS = H // 4
    UNITS = 2 * GROUPS
    E = gate_t.shape[1]
    ED = E - 1
    FC = wd_t.shape[1] // P
    CAP = max(-(-T * 5 // (4 * ED)), 4)
    TB = 4
    FG = B // TB
    W3 = 32
    W3K = 3 * W3
    assert UNITS == 8 and FC == 6 and B % 4 == 0

    def on(q):
        return 0 <= q < PAIRS if isinstance(q, int) else True

    def at(p, first):
        return isinstance(p, int) and p == first

    def shift(p, j, d):
        t = j + d
        return p + t // UNITS, t % UNITS

    def wait(eng, sem, value):
        if not isinstance(value, int) or value > 0:
            eng.wait_ge(sem, value)

    def many(value, most):
        return max(0, min(most, value)) if isinstance(value, int) else value

    def cols(q, n):
        return bass.ds(q * n, n)

    with ExitStack() as ctx:
        def sb(name, shape, dt=F32):
            return ctx.enter_context(nc.sbuf_tensor(name, shape, dt))

        def psum(name, shape):
            return ctx.enter_context(nc.psum_tensor(name, shape, F32))

        def sem(name):
            return ctx.enter_context(nc.semaphore(name))

        x_all = sb("x_all", [P, B, P])
        ctx_all = sb("ctx_all", [P, T])
        wq = sb("wq", [DH, H * P])
        wk = sb("wk", [DH, H * P])
        wv = sb("wv", [P, H * DH])
        wo = sb("wo", [P, H // 2, P])
        bo = sb("bo", [P, P])
        gate = sb("gate", [P, E])
        wg = sb("wg", [P, FC * P])
        wu = sb("wu", [P, FC * P])
        wd = sb("wd", [P, FC, P])
        ctx_hi = sb("ctx_hi", [P, T], F32R)
        ctx_lo = sb("ctx_lo", [P, T], F32R)
        ctxv_hi = sb("ctxv_hi", [P, 2 * P], F32R)
        ctxv_lo = sb("ctxv_lo", [P, 2 * P], F32R)
        a_hi = sb("a_hi", [P, H, P], F32R)
        a_lo = sb("a_lo", [P, H, P], F32R)
        wv_hi = sb("wv_hi", [P, H * DH], F32R)
        wv_lo = sb("wv_lo", [P, H * DH], F32R)
        wg_hi = sb("wg_hi", [P, FC * P], F32R)
        wg_lo = sb("wg_lo", [P, FC * P], F32R)
        wu_hi = sb("wu_hi", [P, FC * P], F32R)
        wu_lo = sb("wu_lo", [P, FC * P], F32R)
        z_hi = sb("z_hi", [P, 2, 4, 2, P], F32R)
        z_lo = sb("z_lo", [P, 2, 4, 2, P], F32R)
        xt_hi = sb("xt_hi", [P, 2, P], F32R)
        xt_lo = sb("xt_lo", [P, 2, P], F32R)
        x2_hi = sb("x2_hi", [P, T], F32R)
        x2_lo = sb("x2_lo", [P, T], F32R)
        stat1 = sb("stat1", [P, 2, 6])
        mv1 = sb("mv1", [P, 2, 2])
        var1 = sb("var1", [P, 2])
        rstd1 = sb("rstd1", [P, 2])
        xn = sb("xn", [P, 2, P])
        xt = sb("xt", [P, 2 * P])
        neg_max = sb("neg_max", [P, 2, 4])
        row_sum = sb("row_sum", [P, 2, 4])
        row_inv = sb("row_inv", [P, 2, 4])
        prob = sb("prob", [P, 2, 4, P])
        prob_n = sb("prob_n", [P, 2, 4, P])
        prob_t = sb("prob_t", [P, 2, 4, P])
        v = sb("v", [P, 2, H * DH])
        ot = sb("ot", [P, 2, 2, P])
        xb = sb("xb", [P, 2, P])
        x1 = sb("x1", [P, 2, P])
        x1_all = sb("x1_all", [P, T])
        stat2 = sb("stat2", [P, 2, 6])
        mv2 = sb("mv2", [P, 2, 2])
        var2 = sb("var2", [P, 2])
        rstd2 = sb("rstd2", [P, 2])
        x2n = sb("x2n", [P, 2, P])
        x2t = sb("x2t", [P, 2 * P])
        logit = sb("logit", [P, 2, E])
        size = sb("size", [P, 2, ED])
        gap = sb("gap", [P, 2, ED, ED])
        big = sb("big", [P, 2, ED, ED])
        keep = sb("keep", [P, 2, ED, ED])
        tie = sb("tie", [P, 2, ED, ED])
        ahead = sb("ahead", [P, 2, ED, ED])
        gap0 = sb("gap0", [P, 2, ED, ED])
        near = sb("near", [P, 2, ED, ED])
        e_gap = sb("e_gap", [P, 2, ED, ED])
        e_near = sb("e_near", [P, 2, ED, ED])
        e_ahead = sb("e_ahead", [P, 2, ED, ED])
        denom = sb("denom", [P, 2, ED])
        rank = sb("rank", [P, 2, ED])
        top = sb("top", [P, 2])
        below = sb("below", [P, 2, ED])
        e_dyn = sb("e_dyn", [P, 2, ED])
        mass = sb("mass", [P, 2, ED])
        total = sb("total", [P, 2])
        small = sb("small", [P, 2, ED])
        valid = sb("valid", [P, 2, ED])
        mult = sb("mult", [P, 2, ED])
        mult_v = sb("mult_v", [P, 2, ED])
        mult_sum = sb("mult_sum", [P, 2])
        mult_inv = sb("mult_inv", [P, 2])
        rw = sb("rw", [P, 2, ED])
        taken = sb("taken", [P, 2, ED], BF16)
        carry = sb("carry", [P, 3, ED], BF16)
        count = sb("count", [P, 2, ED])
        fits = sb("fits", [P, 2, ED])
        shown = sb("shown", [P, 2, ED])
        hidden = sb("hidden", [P, 2, ED])
        masked = sb("masked", [P, 2, E])
        top2 = sb("top2", [P, 2])
        below2 = sb("below2", [P, 2, E])
        e_all = sb("e_all", [P, 2, E])
        total2 = sb("total2", [P, 2])
        total_dyn = sb("total_dyn", [P, 2])
        inv2 = sb("inv2", [P, 2])
        share_dyn = sb("share_dyn", [P, 2])
        gd = sb("gd", [P, 2, ED])
        w = sb("w", [P, 2, E])
        w_rest = sb("w_rest", [P, 2, E])
        w3 = sb("w3", [P, 2, W3K], BF16)
        w3_all = sb("w3_all", [W3K, T], BF16)
        act = sb("act", [P, 2, TB * P])
        gu = sb("gu", [P, 2, TB * P])
        hid = sb("hid", [P, 3, TB * P])
        y = sb("y", [P, 2, TB * P])
        ident = sb("ident", [P, P])
        ident_b = sb("ident_b", [P, P], BF16)
        upto = sb("upto", [P, P], BF16)
        ones = sb("ones", [P, P], BF16)
        first = sb("first", [P, 2, ED, ED])
        pick = sb("pick", [W3K, FC - 1, P], BF16)
        power = sb("power", [P, 2])
        eps = sb("eps", [P, 2])

        z_ps = psum("z_ps", [P, 2, 512])
        s_ps = psum("s_ps", [P, 2, 512])
        t_ps = psum("t_ps", [P, 512])
        o_ps = psum("o_ps", [P, 512])
        acc_ps = psum("acc_ps", [P, 512])
        v_ps = psum("v_ps", [P, 512])
        aux = o_ps[:, 256:512]
        aux_b = aux.bitcast(BF16)

        d_wk, d_wq, d_ctx0, d_ctx, d_x0, d_x, d_wv, d_wo, d_bo, d_gate, d_wg, d_wu, d_wd = (
            sem("d_" + n) for n in "wk wq ctx0 ctx x0 x wv wo bo gate wg wu wd".split())
        zeroed, made = sem("zeroed"), sem("made")
        ctx_split = sem("ctx_split")
        a_mm, a_hi_done, a_lo_done = sem("a_mm"), sem("a_hi_done"), sem("a_lo_done")
        wv_split = sem("wv_split")
        w_split = sem("w_split")
        ctxv_ready = sem("ctxv_ready")
        ln1, ln1_rstd, xn_ready, xt_mm, xt_ready, xt_split = (
            sem(n) for n in "ln1 ln1_rstd xn_ready xt_mm xt_ready xt_split".split())
        z_mm, z_hi_done, z_lo_done = sem("z_mm"), sem("z_hi_done"), sem("z_lo_done")
        s_done, max_done, exp_done, inv_done, norm_done = (
            sem(n) for n in "s_done max_done exp_done inv_done norm_done".split())
        t_done, pt_done, av_done, ot_done, wo_done = (
            sem(n) for n in "t_done pt_done av_done ot_done wo_done".split())
        v_mm, v_ready = sem("v_mm"), sem("v_ready")
        xb_ready, x1_done, x1_kept = sem("xb_ready"), sem("x1_done"), sem("x1_kept")
        ln2, ln2_rstd, x2n_ready, x2_mm, x2t_ready, x2_split = (
            sem(n) for n in "ln2 ln2_rstd x2n_ready x2_mm x2t_ready x2_split".split())
        logit_mm, logit_ready = sem("logit_mm"), sem("logit_ready")
        step, router_exp = sem("step"), sem("router_exp")
        count_mm, count_ready = sem("count_mm"), sem("count_ready")
        w3_mm, w3_ready = sem("w3_mm"), sem("w3_ready")
        g_mm, u_mm, wb_mm, silu_done, gu_done, hid_done, down_done, y_done = (
            sem(n) for n in "g_mm u_mm wb_mm silu_done gu_done hid_done down_done y_done".split())
        stored = [sem(f"stored{k}") for k in range(2)]

        A0, A1, A2, B0, B1, B2 = 5, 10, 23, 26, 34, 45

        with nc.Block() as block:
            @block.sync
            def _(sp):
                x_v = x.rearrange("b t d -> t b d")
                sp.dma_start(wk[:], wk_t).then_inc(d_wk, 16)
                sp.dma_start(ctx_all[:, 0:2 * P], ctx_t[:, 0:2 * P]).then_inc(d_ctx0, 16)
                sp.dma_start(wv[:], w_v).then_inc(d_wv, 16)
                sp.dma_start(ctx_all[:, 2 * P:T], ctx_t[:, 2 * P:T]).then_inc(d_ctx, 16)
                sp.dma_start(x_all[:, 2:B, :], x_v[:, 2:B, :]).then_inc(d_x, 16)
                sp.dma_start(wo[:], w_o.rearrange("(c p) d -> p c d", p=P)).then_inc(d_wo, 16)
                sp.dma_start(wg[:], wg_t).then_inc(d_wg, 16)
                sp.dma_start(wu[:], wu_t).then_inc(d_wu, 16)
                sp.dma_start(wd[:].rearrange("p c d -> p (c d)"), wd_t).then_inc(d_wd, 16)
                out_v = out.rearrange("b t d -> t b d")
                for g in range(FG):
                    sp.wait_ge(y_done, g + 1)
                    sp.dma_start(out_v[:, TB * g:TB * g + TB, :],
                                 y[:, g % 2, :].rearrange("p (b d) -> p b d", b=TB)).then_inc(stored[g % 2], 16)
                for k in range(2):
                    sp.wait_ge(stored[k], 16 * (FG // 2))

            @block.gpsimd
            def _(pool):
                nc.gpsimd.memset(ident[:], 0.0).then_inc(zeroed, 1)
                nc.gpsimd.memset(ident_b[:], 0.0).then_inc(zeroed, 1)
                nc.gpsimd.memset(upto[:], 0.0).then_inc(zeroed, 1)
                nc.gpsimd.memset(first[:], 0.0).then_inc(zeroed, 1)
                nc.gpsimd.memset(pick[:], 0.0).then_inc(zeroed, 1)
                nc.gpsimd.memset(w3[:], 0.0).then_inc(zeroed, 1)
                nc.gpsimd.memset(carry[:], 0.0).then_inc(zeroed, 1)
                nc.gpsimd.memset(power[:], -0.5).then_inc(zeroed, 1)
                nc.gpsimd.memset(ones[:], 1.0).then_inc(zeroed, 1)
                nc.gpsimd.memset(eps[:], EPS).then_inc(zeroed, 1)
                pool.wait_ge(zeroed, 10)
                for m in (ident, ident_b):
                    nc.gpsimd.affine_select(out=m[:], in_=m[:], compare_op=ALU.not_equal, fill=1.0, base=0,
                                            pattern=[[-1, P]], channel_multiplier=1).then_inc(made, 1)
                nc.gpsimd.affine_select(out=upto[:], in_=upto[:], compare_op=ALU.is_gt, fill=1.0, base=0,
                                        pattern=[[-1, P]], channel_multiplier=1).then_inc(made, 1)
                nc.gpsimd.affine_select(out=first[:], in_=first[:], compare_op=ALU.is_ge, fill=1.0, base=0,
                                        pattern=[[0, 2], [-1, ED], [1, ED]], channel_multiplier=0).then_inc(made, 1)
                for part in range(3):
                    pool.wait_ge(made, 4 + 2 * part)
                    rows = pick[W3 * part:W3 * part + W3]
                    dyn = rows[:, 0:ED // 2, :].rearrange("r c (h i) -> r c h i", h=2)
                    nc.gpsimd.affine_select(out=dyn, in_=dyn, compare_op=ALU.not_equal, fill=1.0, base=0,
                                            pattern=[[-2, ED // 2], [-1, 2], [0, DH]],
                                            channel_multiplier=1).then_inc(made, 1)
                    shared = rows[:, ED // 2, :]
                    nc.gpsimd.affine_select(out=shared, in_=shared, compare_op=ALU.not_equal, fill=1.0, base=-ED,
                                            pattern=[[0, P]], channel_multiplier=1).then_inc(made, 1)

                pool.wait_ge(made, 10)

                def split_weights(src, hi, lo, landed, n):
                    pool.wait_ge(landed, 16)
                    nc.gpsimd.tensor_copy(hi[:], src[:]).then_inc(w_split, 1)
                    pool.wait_ge(w_split, n + 1)
                    nc.gpsimd.tensor_tensor(lo[:], src[:], hi[:].bitcast(F32), ALU.subtract).then_inc(w_split, 1)

                def slot(p, j):
                    if j == 2 and on(p + 1):
                        q = p + 1
                        wait(pool, ln1, 4 * q + 4)
                        nc.gpsimd.tensor_tensor(var1[:], mv1[:, :, 1], eps[:], ALU.add).then_inc(ln1_rstd, 1)
                        wait(pool, ln1_rstd, 2 * q + 1)
                        nc.gpsimd.tensor_tensor(rstd1[:], var1[:], power[:], ALU.pow).then_inc(ln1_rstd, 1)
                    if j == 5 and on(p - 1):
                        q = p - 1
                        wait(pool, ln2, 4 * q + 4)
                        nc.gpsimd.tensor_tensor(var2[:], mv2[:, :, 1], eps[:], ALU.add).then_inc(ln2_rstd, 1)
                        wait(pool, ln2_rstd, 2 * q + 1)
                        nc.gpsimd.tensor_tensor(rstd2[:], var2[:], power[:], ALU.pow).then_inc(ln2_rstd, 1)
                    q, u = shift(p, j, -1)
                    if on(q):
                        n = UNITS * q + u
                        wait(pool, inv_done, n + 1)
                        wait(pool, t_done, n - 1)
                        nc.gpsimd.tensor_tensor(prob_n[:, u % 2], prob[:, u % 2],
                                                row_inv[:, u % 2, :].unsqueeze(2).to_broadcast([P, 4, P]),
                                                ALU.mult).then_inc(norm_done, 1)
                    if j == 6 and on(p):
                        if at(p, 0):
                            pool.wait_ge(d_bo, 16)
                            pool.wait_ge(d_x0, 16)
                            pool.wait_ge(d_x, 16)
                        wait(pool, x1_done, p)
                        nc.gpsimd.tensor_tensor(xb[:], x_all[:, cols(p, 2), :],
                                                bo[:].unsqueeze(1).to_broadcast([P, 2, P]),
                                                ALU.add).then_inc(xb_ready, 1)
                    if j == 5 and on(p + 1):
                        q = p + 1
                        if at(q, 0) or at(q, 1):
                            pool.wait_ge(ctx_split, 2 * q + 2)
                        wait(pool, v_mm, 4 * q)
                        nc.gpsimd.tensor_copy(ctxv_hi[:], ctx_hi[:, cols(q, 2 * P)]).then_inc(ctxv_ready, 1)
                        nc.gpsimd.tensor_copy(ctxv_lo[:], ctx_lo[:, cols(q, 2 * P)]).then_inc(ctxv_ready, 1)
                    if j == 4 and on(p - 1):
                        wait(pool, x1_done, p)
                        nc.gpsimd.tensor_copy(x1_all[:, cols(p - 1, 2 * P)],
                                              x1[:].rearrange("p b d -> p (b d)")).then_inc(x1_kept, 1)
                    if j == 7 and on(p - 1):
                        q = p - 1
                        wait(pool, x2t_ready, q + 1)
                        nc.gpsimd.tensor_copy(x2_hi[:, cols(q, 2 * P)], x2t[:]).then_inc(x2_split, 1)
                        wait(pool, x2_split, 2 * q + 1)
                        nc.gpsimd.tensor_tensor(x2_lo[:, cols(q, 2 * P)], x2t[:],
                                                x2_hi[:, cols(q, 2 * P)].bitcast(F32),
                                                ALU.subtract).then_inc(x2_split, 1)
                    if at(p, 0) and j == 3:
                        split_weights(wg, wg_hi, wg_lo, d_wg, 0)
                    if at(p, 1) and j == 3:
                        split_weights(wu, wu_hi, wu_lo, d_wu, 2)

                for p in (-1, 0, 1):
                    for j in range(UNITS):
                        slot(p, j)
                with pool.Fori(2, PAIRS - 1) as p:
                    for j in range(UNITS):
                        slot(p, j)
                for p in (PAIRS - 1, PAIRS, PAIRS + 1):
                    for j in range(UNITS):
                        slot(p, j)

            @block.scalar
            def _(sc):
                sc.dma_start(wq[:], wq_t).then_inc(d_wq, 16)
                sc.dma_start(x_all[:, 0:2, :], x.rearrange("b t d -> t b d")[:, 0:2, :]).then_inc(d_x0, 16)
                sc.dma_start(bo[:], b_o.to_broadcast([P, P])).then_inc(d_bo, 16)
                sc.dma_start(gate[:], gate_t).then_inc(d_gate, 16)
                for g in range(GROUPS):
                    sc.wait_ge(a_mm, g + 1)
                    bank = (z_ps, s_ps)[g // 2][:, g % 2, :]
                    nc.scalar.activation(a_hi[:, 4 * g:4 * g + 4, :].rearrange("p h d -> p (h d)"), bank, ACT.Copy,
                                         scale=DH ** -0.5).then_inc(a_hi_done, 1)
                sc.wait_ge(d_wv, 16)
                nc.scalar.activation(wv_hi[:], wv[:], ACT.Copy).then_inc(wv_split, 1)

                def slot(p, j):
                    if j == 1 and on(p - 2):
                        wait(sc, step, B2 * (p - 2) + A0)
                        nc.scalar.activation(e_gap[:], gap0[:], ACT.Exp, scale=-1.0).then_inc(router_exp, 1)
                        nc.scalar.activation(e_dyn[:], below[:], ACT.Exp).then_inc(router_exp, 1)
                    if j == 6 and on(p - 2):
                        wait(sc, step, B2 * (p - 2) + B1)
                        nc.scalar.activation(e_all[:], below2[:], ACT.Exp).then_inc(router_exp, 1)
                    q, z = shift(p, j, 3)
                    if on(q):
                        wait(sc, z_mm, UNITS * q + z + 1)
                        wait(sc, s_done, UNITS * q + 2 * (z // 2) - 2)
                        nc.scalar.activation(
                            z_hi[:, (z // 2) % 2, 2 * (z % 2):2 * (z % 2) + 2].rearrange("p h b m -> p (h b m)"),
                            z_ps[:, z % 2, :], ACT.Copy).then_inc(z_hi_done, 1)
                    if on(p):
                        n = UNITS * p + j
                        wait(sc, max_done, n + 1)
                        wait(sc, norm_done, n - 1)
                        for h in range(4):
                            last = nc.scalar.activation(
                                prob[:, j % 2, h, :], s_ps[:, j % 2, h * P:(h + 1) * P], ACT.Exp,
                                bias=neg_max[:, j % 2, h:h + 1], accum_out=row_sum[:, j % 2, h:h + 1])
                        last.then_inc(exp_done, 1)
                    q, u = shift(p, j, -3)
                    if on(q):
                        wait(sc, av_done, UNITS * q + u + 1)
                    if j == 3 and on(p - 2):
                        wait(sc, count_mm, p - 1)
                        nc.scalar.activation(count[:].rearrange("p b e -> p (b e)"), aux[:, 0:2 * ED],
                                             ACT.Copy).then_inc(count_ready, 1)
                    if j == 5 and on(p + 1):
                        wait(sc, xt_mm, p + 2)
                        wait(sc, xt_split, 4 * (p + 1))
                        nc.scalar.activation(xt[:], aux, ACT.Copy).then_inc(xt_ready, 1)
                    if j == 6 and on(p - 1):
                        wait(sc, x2_mm, p)
                        wait(sc, x2_split, 2 * (p - 1))
                        wait(sc, logit_mm, p - 1)
                        nc.scalar.activation(x2t[:], aux, ACT.Copy).then_inc(x2t_ready, 1)
                    if j == 7 and on(p - 1):
                        wait(sc, logit_mm, p)
                        wait(sc, step, B2 * (p - 1))
                        nc.scalar.activation(logit[:].rearrange("p b e -> p (b e)"), aux[:, 0:2 * E],
                                             ACT.Copy).then_inc(logit_ready, 1)
                    if j == 7 and on(p - 2):
                        wait(sc, w3_mm, p - 1)
                        nc.scalar.activation(w3_all[:, cols(p - 2, 2 * P)], aux_b[0:W3K, P:P + 2 * P],
                                             ACT.Copy).then_inc(w3_ready, 1)
                    if on(q):
                        n = UNITS * q + u
                        wait(sc, wo_done, n - 1)
                        nc.scalar.activation(ot[:, u % 2].rearrange("p c t -> p (c t)"), o_ps[:, 0:256],
                                             ACT.Copy).then_inc(ot_done, 1)
                    q, vi = {7: (p + 1, 0), 0: (p, 1), 3: (p, 2), 4: (p, 3)}.get(j, (PAIRS, 0))
                    if on(q):
                        wait(sc, v_mm, 4 * q + vi + 1)
                        wait(sc, av_done, UNITS * (q - 1) + (2, 3, 6, 7)[vi] + 1)
                        nc.scalar.activation(v[:, vi % 2, (vi // 2) * 512:(vi // 2) * 512 + 512], v_ps[:],
                                             ACT.Copy).then_inc(v_ready, 1)

                for p in (-1, 0, 1):
                    for j in range(UNITS):
                        slot(p, j)
                with sc.Fori(2, PAIRS - 1) as p:
                    for j in range(UNITS):
                        slot(p, j)
                for p in (PAIRS - 1, PAIRS, PAIRS + 1):
                    for j in range(UNITS):
                        slot(p, j)

                for g in range(FG):
                    for c in range(FC):
                        n = FC * g + c
                        sc.wait_ge(g_mm, n + 1)
                        wait(sc, gu_done, n - 1)
                        nc.scalar.activation(act[:, c % 2, :], z_ps[:, c % 2, :], ACT.Silu).then_inc(silu_done, 1)

            @block.vector
            def _(ve):
                ve.wait_ge(d_ctx0, 16)
                nc.vector.tensor_copy(ctx_hi[:, 0:2 * P], ctx_all[:, 0:2 * P]).then_inc(ctx_split, 1)
                ve.wait_ge(ctx_split, 1)
                nc.vector.tensor_tensor(ctx_lo[:, 0:2 * P], ctx_all[:, 0:2 * P],
                                        ctx_hi[:, 0:2 * P].bitcast(F32), ALU.subtract).then_inc(ctx_split, 1)
                for g in range(GROUPS):
                    ve.wait_ge(a_hi_done, g + 1)
                    bank = (z_ps, s_ps)[g // 2][:, g % 2, :]
                    nc.vector.scalar_tensor_tensor(
                        a_lo[:, 4 * g:4 * g + 4, :].rearrange("p h d -> p (h d)"), bank, DH ** -0.5,
                        a_hi[:, 4 * g:4 * g + 4, :].rearrange("p h d -> p (h d)").bitcast(F32),
                        ALU.mult, ALU.subtract).then_inc(a_lo_done, 1)
                ve.wait_ge(wv_split, 1)
                nc.vector.tensor_tensor(wv_lo[:], wv[:], wv_hi[:].bitcast(F32), ALU.subtract).then_inc(wv_split, 1)

                class Steps:

                    def __init__(self, q, start):
                        self.before, self.n = B2 * q, start

                    def done(self, ins):
                        self.n += 1
                        ins.then_inc(step, 1)

                    def wait_all(self):
                        wait(ve, step, self.before + self.n)

                def flat(a):
                    return a[:].rearrange("p b j i -> p (b j i)")

                def wide(a, n=ED):
                    return a[:].unsqueeze(2).to_broadcast([P, 2, n])

                def of_j(a):
                    return a.unsqueeze(3).to_broadcast([P, 2, ED, ED])

                def of_i(a):
                    return a.unsqueeze(2).to_broadcast([P, 2, ED, ED])

                tensor, two, scale, red = (nc.vector.tensor_tensor, nc.vector.scalar_tensor_tensor,
                                           nc.vector.tensor_scalar, nc.vector.tensor_reduce)
                s = logit[:, :, 0:ED]

                def gaps(q):
                    r = Steps(q, 0)
                    wait(ve, logit_ready, q + 1)
                    r.done(tensor(gap[:], of_j(s), of_i(s), ALU.subtract))
                    r.done(two(size[:], s, -1.0, s, ALU.mult, ALU.max))
                    r.done(red(top[:], s, X, ALU.max))
                    r.wait_all()
                    r.done(scale(flat(gap0), flat(gap), 0.0, None, ALU.max))
                    r.done(tensor(below[:], s, wide(top), ALU.subtract))
                    assert r.n == A0

                def orders(q):
                    r = Steps(q, A0)
                    r.wait_all()
                    r.done(tensor(big[:], of_j(size[:]), of_i(size[:]), ALU.max))
                    r.done(two(flat(tie), flat(gap), 0.0, flat(first), ALU.is_equal, ALU.mult))
                    r.wait_all()
                    r.done(two(flat(ahead), flat(gap), 0.0, flat(tie), ALU.is_lt, ALU.add))
                    r.done(two(flat(keep), flat(big), JITTER, flat(gap), ALU.mult, ALU.is_ge))
                    r.wait_all()
                    r.done(two(flat(near), flat(ahead), 0.5, flat(keep), ALU.is_lt, ALU.mult))
                    assert r.n == A1

                def choices(q):
                    r = Steps(q, A1)
                    r.wait_all()
                    wait(ve, router_exp, 3 * q + 2)
                    r.done(tensor(flat(e_near), flat(e_gap), flat(near), ALU.mult))
                    r.done(red(rank[:], ahead[:], X, ALU.add))
                    r.done(red(total[:], e_dyn[:], X, ALU.add))
                    r.done(tensor(e_ahead[:], ahead[:], of_i(e_dyn[:]), ALU.mult))
                    r.wait_all()
                    r.done(red(denom[:], e_near[:], X, ALU.add))
                    r.done(red(mass[:], e_ahead[:], X, ALU.add))
                    r.wait_all()
                    r.done(nc.vector.reciprocal(mult[:], denom[:]))
                    r.done(two(small[:], wide(total), TOP_P, mass[:], ALU.mult, ALU.is_gt))
                    r.wait_all()
                    r.done(two(valid[:], rank[:], float(TOP_K), small[:], ALU.is_lt, ALU.mult))
                    r.wait_all()
                    r.done(nc.vector.tensor_copy(taken[:], valid[:]))
                    r.done(tensor(mult_v[:], mult[:], valid[:], ALU.mult))
                    r.done(nc.vector.tensor_copy(carry[:, 0, :], carry[:, 2, :]))
                    r.wait_all()
                    r.done(tensor(carry[:, 1, :], carry[:, 0, :], taken[:, 0, :], ALU.add))
                    assert r.n == A2

                def capacity(q):
                    r = Steps(q, A2)
                    r.wait_all()
                    r.done(tensor(carry[:, 2, :], carry[:, 1, :], taken[:, 1, :], ALU.add))
                    r.done(red(mult_sum[:], mult_v[:], X, ALU.add))
                    wait(ve, count_ready, q + 1)
                    r.done(two(fits[:], count[:], float(CAP), valid[:], ALU.is_le, ALU.mult))
                    assert r.n == B0

                def hiding(q):
                    r = Steps(q, B0)
                    r.wait_all()
                    r.done(tensor(shown[:], s, fits[:], ALU.mult))
                    r.done(scale(hidden[:], fits[:], 1.0, HIDE, ALU.subtract, ALU.mult))
                    r.done(nc.vector.tensor_copy(masked[:, :, ED:E], logit[:, :, ED:E]))
                    r.done(nc.vector.reciprocal(mult_inv[:], mult_sum[:]))
                    r.wait_all()
                    r.done(tensor(masked[:, :, 0:ED], shown[:], hidden[:], ALU.add))
                    r.done(tensor(rw[:], mult_v[:], wide(mult_inv), ALU.mult))
                    r.wait_all()
                    r.done(red(top2[:], masked[:], X, ALU.max))
                    r.wait_all()
                    r.done(tensor(below2[:], masked[:], wide(top2, E), ALU.subtract))
                    assert r.n == B1

                def weights(q):
                    r = Steps(q, B1)
                    wait(ve, router_exp, 3 * q + 3)
                    r.wait_all()
                    r.done(red(total2[:], e_all[:], X, ALU.add))
                    r.done(red(total_dyn[:], e_all[:, :, 0:ED], X, ALU.add))
                    r.wait_all()
                    r.done(nc.vector.reciprocal(inv2[:], total2[:]))
                    r.wait_all()
                    r.done(tensor(share_dyn[:], total_dyn[:], inv2[:], ALU.mult))
                    r.done(tensor(w[:, :, ED:E], e_all[:, :, ED:E], wide(inv2, 1), ALU.mult))
                    r.wait_all()
                    r.done(tensor(gd[:], rw[:], wide(share_dyn), ALU.mult))
                    r.wait_all()
                    r.done(tensor(w[:, :, 0:ED], gd[:], fits[:], ALU.mult))
                    r.wait_all()
                    if isinstance(q, int):
                        wait(ve, w3_mm, q)
                    r.done(nc.vector.tensor_copy(w3[:, :, 0:E], w[:]))
                    r.wait_all()
                    r.done(tensor(w_rest[:], w[:], w3[:, :, 0:E], ALU.subtract))
                    r.wait_all()
                    r.done(nc.vector.tensor_copy(w3[:, :, W3:W3 + E], w_rest[:]))
                    r.wait_all()
                    r.done(tensor(w3[:, :, 2 * W3:2 * W3 + E], w_rest[:], w3[:, :, W3:W3 + E], ALU.subtract))
                    assert r.n == B2

                def slot(p, j):
                    if j == 1 and on(p + 1):
                        q = p + 1
                        if at(q, 0):
                            ve.wait_ge(d_x0, 16)
                        if at(q, 1):
                            ve.wait_ge(d_x, 16)
                        for b in range(2):
                            nc.vector.bn_stats(stat1[:, b, :], x_all[:, cols(2 * q + b, 1), :]
                                               .rearrange("p b d -> p (b d)")).then_inc(ln1, 1)
                        wait(ve, ln1, 4 * q + 2)
                        wait(ve, ln1_rstd, 2 * q)
                    if j == 3 and on(p + 1):
                        q = p + 1
                        wait(ve, ln1_rstd, 2 * q + 2)
                        wait(ve, xt_mm, q)
                        for b in range(2):
                            nc.vector.tensor_scalar(
                                xn[:, b, :], x_all[:, cols(2 * q + b, 1), :].rearrange("p b d -> p (b d)"),
                                mv1[:, b, 0:1], rstd1[:, b:b + 1], ALU.subtract, ALU.mult).then_inc(xn_ready, 1)
                    q, b = (p + 1, 0) if j == 7 else (p, 1)
                    if j in (7, 0) and on(q):
                        wait(ve, xt_ready, q + 1)
                        wait(ve, s_done, UNITS * q - 1 + b)
                        nc.vector.tensor_copy(xt_hi[:, b, :], xt[:, b * P:(b + 1) * P]).then_inc(xt_split, 1)
                        wait(ve, xt_split, 4 * q + 2 * b + 1)
                        nc.vector.tensor_tensor(xt_lo[:, b, :], xt[:, b * P:(b + 1) * P],
                                                xt_hi[:, b, :].bitcast(F32), ALU.subtract).then_inc(xt_split, 1)
                    if j == 4 and on(p - 1):
                        q = p - 1
                        wait(ve, wo_done, UNITS * q + UNITS)
                        wait(ve, xb_ready, q + 1)
                        wait(ve, x1_kept, q)
                        nc.vector.tensor_tensor(x1[:].rearrange("p b d -> p (b d)"), acc_ps[:, 0:2 * P],
                                                xb[:].rearrange("p b d -> p (b d)"), ALU.add).then_inc(x1_done, 1)
                        wait(ve, x1_done, q + 1)
                        for b in range(2):
                            nc.vector.bn_stats(stat2[:, b, :], x1[:, b, :]).then_inc(ln2, 1)
                        wait(ve, ln2, 4 * q + 2)
                    q, u = shift(p, j, -1)
                    if on(q):
                        wait(ve, exp_done, UNITS * q + u + 1)
                        nc.vector.reciprocal(row_inv[:, u % 2, :], row_sum[:, u % 2, :]).then_inc(inv_done, 1)
                    if on(p):
                        wait(ve, s_done, UNITS * p + j + 1)
                        nc.vector.tensor_reduce(neg_max[:, j % 2, :],
                                                s_ps[:, j % 2, :].rearrange("p (h m) -> p h m", h=4),
                                                X, ALU.max, negate=True).then_inc(max_done, 1)
                    if j == 1 and on(p + 1):
                        for b in range(2):
                            nc.vector.bn_aggr(mv1[:, b, :], stat1[:, b, :]).then_inc(ln1, 1)
                    if j == 4 and on(p - 1):
                        for b in range(2):
                            nc.vector.bn_aggr(mv2[:, b, :], stat2[:, b, :]).then_inc(ln2, 1)
                    if j == 5 and on(p - 1):
                        q = p - 1
                        wait(ve, ln2_rstd, 2 * q + 2)
                        for b in range(2):
                            nc.vector.tensor_scalar(x2n[:, b, :], x1[:, b, :], mv2[:, b, 0:1], rstd2[:, b:b + 1],
                                                    ALU.subtract, ALU.mult).then_inc(x2n_ready, 1)
                    if on(p - 2):
                        if j == 0:
                            if at(p, 2):
                                ve.wait_ge(made, 10)
                            gaps(p - 2)
                        if j == 1:
                            orders(p - 2)
                        if j == 2:
                            choices(p - 2)
                        if j == 4:
                            capacity(p - 2)
                        if j == 5:
                            hiding(p - 2)
                        if j == 6:
                            weights(p - 2)
                    q, u = shift(p, j, -2)
                    if on(q):
                        n = UNITS * q + u
                        wait(ve, t_done, n + 1)
                        wait(ve, av_done, n - 1)
                        nc.vector.tensor_copy(prob_t[:, u % 2].rearrange("p h t -> p (h t)"),
                                              t_ps[:]).then_inc(pt_done, 1)
                    q, z = shift(p, j, 3)
                    if on(q):
                        wait(ve, z_hi_done, UNITS * q + z + 1)
                        zh = z_hi[:, (z // 2) % 2, 2 * (z % 2):2 * (z % 2) + 2].rearrange("p h b m -> p (h b m)")
                        zl = z_lo[:, (z // 2) % 2, 2 * (z % 2):2 * (z % 2) + 2].rearrange("p h b m -> p (h b m)")
                        nc.vector.tensor_tensor(zl, z_ps[:, z % 2, :], zh.bitcast(F32),
                                                ALU.subtract).then_inc(z_lo_done, 1)
                    if at(p, 0) and j == 2:
                        ve.wait_ge(d_ctx, 16)
                        nc.vector.tensor_copy(ctx_hi[:, 2 * P:T], ctx_all[:, 2 * P:T]).then_inc(ctx_split, 1)
                        ve.wait_ge(ctx_split, 3)
                        nc.vector.tensor_tensor(ctx_lo[:, 2 * P:T], ctx_all[:, 2 * P:T],
                                                ctx_hi[:, 2 * P:T].bitcast(F32), ALU.subtract).then_inc(ctx_split, 1)

                for p in (-1, 0, 1):
                    for j in range(UNITS):
                        slot(p, j)
                with ve.Fori(2, PAIRS - 1) as p:
                    for j in range(UNITS):
                        slot(p, j)
                for p in (PAIRS - 1, PAIRS, PAIRS + 1):
                    for j in range(UNITS):
                        slot(p, j)

                for g in range(FG):
                    def residual(g):
                        wait(ve, down_done, FC * g + FC)
                        wait(ve, stored[g % 2], 16 * (g // 2))
                        nc.vector.tensor_tensor(y[:, g % 2, :], acc_ps[:], x1_all[:, cols(g, TB * P)],
                                                ALU.add).then_inc(y_done, 1)

                    for c in range(FC):
                        n = FC * g + c
                        ve.wait_ge(silu_done, n + 1)
                        ve.wait_ge(u_mm, n + 1)
                        nc.vector.tensor_tensor(gu[:, c % 2, :], s_ps[:, c % 2, :], act[:, c % 2, :],
                                                ALU.mult).then_inc(gu_done, 1)
                        ve.wait_ge(wb_mm, n + 1)
                        ve.wait_ge(gu_done, n + 1)
                        wait(ve, down_done, n - 2)
                        wbank = t_ps if c % 2 else v_ps
                        nc.vector.tensor_tensor(hid[:, c % 3, :], wbank[:], gu[:, c % 2, :],
                                                ALU.mult).then_inc(hid_done, 1)
                        if c == 1 and g > 0:
                            residual(g - 1)
                residual(FG - 1)

            @block.tensor
            def _(pe):
                mm = nc.tensor.matmul
                pe.wait_ge(d_wk, 16)
                pe.wait_ge(d_wq, 16)
                for g in range(GROUPS):
                    for h in range(4 * g, 4 * g + 4):
                        bank = (z_ps, s_ps)[g // 2][:, g % 2, :]
                        last = mm(bank[:, (h % 4) * P:(h % 4) * P + P], wk[:, h * P:(h + 1) * P],
                                  wq[:, h * P:(h + 1) * P], start=True, stop=True)
                    last.then_inc(a_mm, 1)

                def split_mm(out, l_hi, l_lo, r_hi, r_lo):
                    mm(out, l_lo, r_hi, start=True, stop=False)
                    mm(out, l_hi, r_lo, start=False, stop=False)
                    return mm(out, l_hi, r_hi, start=False, stop=True)

                def slot(p, j):
                    if on(p):
                        g, b = j // 2, j % 2
                        wait(pe, z_lo_done, UNITS * p + 2 * g + 2)
                        wait(pe, xt_split, 4 * p + 2 * b + 2)
                        wait(pe, exp_done, UNITS * p + j - 1)
                        split_mm(s_ps[:, j % 2, :].rearrange("p (h m) -> p h m", h=4), xt_hi[:, b, :], xt_lo[:, b, :],
                                 z_hi[:, g % 2, :, b, :], z_lo[:, g % 2, :, b, :]).then_inc(s_done, 1)
                    q, z = shift(p, j, 3)
                    if on(q):
                        if at(q, 0):
                            pe.wait_ge(a_lo_done, 1 + z // 2 if z > 2 else GROUPS)
                            pe.wait_ge(ctx_split, 2)
                        if at(q, 1) and z == 0:
                            pe.wait_ge(ctx_split, 4)
                        wait(pe, z_lo_done, UNITS * q + z - 1)
                        for hh in range(2):
                            h = 2 * z + hh
                            last = split_mm(z_ps[:, z % 2, hh * 256:hh * 256 + 256], a_hi[:, h, :], a_lo[:, h, :],
                                            ctx_hi[:, cols(q, 2 * P)], ctx_lo[:, cols(q, 2 * P)])
                        last.then_inc(z_mm, 1)
                    q, u = shift(p, j, -2)
                    if on(q):
                        n = UNITS * q + u
                        if at(n, 0):
                            pe.wait_ge(made, 1)
                        wait(pe, norm_done, n + 1)
                        wait(pe, pt_done, n)
                        for h in range(4):
                            last = nc.tensor.transpose(t_ps[:, h * P:(h + 1) * P], prob_n[:, u % 2, h, :], ident[:])
                        last.then_inc(t_done, 1)

                    def o_bank_free():
                        wait(pe, ot_done, many(UNITS * p + j - 3, UNITS * PAIRS))
                        if isinstance(p, int):
                            wait(pe, count_ready, many(p - 1 - (j <= 3), PAIRS))
                            wait(pe, xt_ready, many(p + 2 - (j <= 5), PAIRS))
                            wait(pe, x2t_ready, many(p - (j <= 6), PAIRS))
                            wait(pe, logit_ready, many(p - 1, PAIRS))
                            wait(pe, w3_ready, many(p - 2, PAIRS))

                    if j == 3 and on(p - 2):
                        o_bank_free()
                        wait(pe, step, B2 * (p - 2) + A2)
                        mm(aux[:, 0:2 * ED], upto[:], taken[:].rearrange("p b e -> p (b e)"), start=True, stop=False)
                        mm(aux[:, 0:2 * ED], ones[:], carry[:, 0:2, :].rearrange("p b e -> p (b e)"),
                           start=False, stop=True).then_inc(count_mm, 1)
                    if j == 5 and on(p + 1):
                        o_bank_free()
                        if at(p, -1):
                            pe.wait_ge(made, 1)
                        wait(pe, xn_ready, 2 * (p + 1) + 2)
                        for b in range(2):
                            last = nc.tensor.transpose(aux[:, b * P:(b + 1) * P], xn[:, b, :], ident[:])
                        last.then_inc(xt_mm, 1)
                    if j == 6 and on(p - 1):
                        o_bank_free()
                        wait(pe, x2n_ready, 2 * p)
                        for b in range(2):
                            last = nc.tensor.transpose(aux[:, b * P:(b + 1) * P], x2n[:, b, :], ident[:])
                        last.then_inc(x2_mm, 1)
                    if j == 7 and (on(p - 1) or on(p - 2)):
                        o_bank_free()
                    if j == 7 and on(p - 2):
                        wait(pe, step, B2 * (p - 1))
                        for b in range(2):
                            last = nc.tensor.transpose(aux_b[0:W3K, P + b * P:2 * P + b * P], w3[:, b, :], ident_b[:])
                        last.then_inc(w3_mm, 1)
                    if j == 7 and on(p - 1):
                        if at(p, 1):
                            pe.wait_ge(d_gate, 16)
                        wait(pe, x2t_ready, p)
                        for b in range(2):
                            last = mm(aux[:, b * E:(b + 1) * E], x2t[:, b * P:(b + 1) * P], gate[:],
                                      start=True, stop=True)
                        last.then_inc(logit_mm, 1)
                    q, u = shift(p, j, -3)
                    if on(q):
                        g, b = u // 2, u % 2
                        o_bank_free()
                        wait(pe, pt_done, UNITS * q + u + 1)
                        wait(pe, v_ready, 4 * q + 2 * (g // 2) + b + 1)
                        for h in range(4):
                            half = (h % 2) * DH
                            last = mm(o_ps[half:half + DH, (h // 2) * P:(h // 2) * P + P],
                                      v[:, b, (4 * g + h) * DH:(4 * g + h + 1) * DH], prob_t[:, u % 2, h, :],
                                      start=True, stop=True)
                        last.then_inc(av_done, 1)
                    q, u = shift(p, j, -4)
                    if on(q):
                        g, b = u // 2, u % 2
                        if at(q, 0) and u == 0:
                            pe.wait_ge(d_wo, 16)
                        wait(pe, ot_done, UNITS * q + u + 1)
                        if u == 0:
                            wait(pe, x1_done, q)
                        for c in range(2):
                            last = mm(acc_ps[:, b * P:(b + 1) * P], ot[:, u % 2, c, :], wo[:, 2 * g + c, :],
                                      start=(u == 0 and c == 0), stop=(g == GROUPS - 1 and c == 1),
                                      skip_group_check=True)
                        last.then_inc(wo_done, 1)
                    q, vi = {7: (p + 1, 0), 0: (p, 1), 3: (p, 2), 4: (p, 3)}.get(j, (PAIRS, 0))
                    if on(q):
                        b, half = vi % 2, (vi // 2) * 512
                        if at(p, -1):
                            pe.wait_ge(wv_split, 2)
                        wait(pe, ctxv_ready, 2 * q + 2)
                        wait(pe, v_ready, 4 * q + vi)
                        split_mm(v_ps[:], ctxv_hi[:, b * P:(b + 1) * P], ctxv_lo[:, b * P:(b + 1) * P],
                                 wv_hi[:, half:half + 512], wv_lo[:, half:half + 512]).then_inc(v_mm, 1)

                for p in (-1, 0, 1):
                    for j in range(UNITS):
                        slot(p, j)
                with pe.Fori(2, PAIRS - 1) as p:
                    for j in range(UNITS):
                        slot(p, j)
                for p in (PAIRS - 1, PAIRS, PAIRS + 1):
                    for j in range(UNITS):
                        slot(p, j)

                def project(n, g, c):
                    wait(pe, hid_done, n + 1)
                    if c == 0:
                        wait(pe, y_done, g)
                    for tile in range(TB):
                        last = mm(acc_ps[:, tile * P:(tile + 1) * P], hid[:, c % 3, tile * P:(tile + 1) * P],
                                  wd[:, c, :], start=(c == 0 and tile == 0), stop=(c == FC - 1),
                                  skip_group_check=True)
                    last.then_inc(down_done, 1)

                LAG = 2
                pe.wait_ge(w_split, 4)
                pe.wait_ge(d_wd, 16)
                pe.wait_ge(x1_done, PAIRS)
                for g in range(FG):
                    tok = cols(g, TB * P)
                    pe.wait_ge(x2_split, min(2 * TB // 2 * (g + 1), 2 * PAIRS))
                    for c in range(FC):
                        n = FC * g + c
                        unit = slice(c * P, (c + 1) * P)
                        wait(pe, silu_done, n - 1)
                        split_mm(z_ps[:, c % 2, :], wg_hi[:, unit], wg_lo[:, unit],
                                 x2_hi[:, tok], x2_lo[:, tok]).then_inc(g_mm, 1)
                        wait(pe, gu_done, n - 1)
                        split_mm(s_ps[:, c % 2, :], wu_hi[:, unit], wu_lo[:, unit],
                                 x2_hi[:, tok], x2_lo[:, tok]).then_inc(u_mm, 1)
                        if c == 0:
                            pe.wait_ge(w3_ready, TB // 2 * (g + 1))
                        wait(pe, hid_done, n - 1)
                        mm((t_ps if c % 2 else v_ps)[:], pick[:, min(c, ED // 2), :], w3_all[:, tok],
                           start=True, stop=True).then_inc(wb_mm, 1)
                        if n >= LAG:
                            project(n - LAG, (n - LAG) // FC, (n - LAG) % FC)
                for n in range(FC * FG - LAG, FC * FG):
                    project(n, n // FC, n % FC)


def kernel(x, ctx_1024, L0_xattn_W_q, L0_xattn_W_k, L0_xattn_W_v, L0_xattn_W_o, L0_xattn_b_o, L0_ffn_gate_w,
           L0_ffn_dyn_gate_w, L0_ffn_dyn_up_w, L0_ffn_dyn_down_w, L0_ffn_sh_gate_w, L0_ffn_sh_up_w,
           L0_ffn_sh_down_w):
    import numpy as np
    import concourse.bacc as bacc
    from concourse.bass_utils import run_bass_kernel_spmd

    def lay(a):
        return np.ascontiguousarray(a)

    x, ctx = np.asarray(x), np.asarray(ctx_1024)
    D = x.shape[-1]
    inner = L0_xattn_W_q.shape[1]
    heads = inner // DH

    def by_head(wt):
        return lay(np.asarray(wt).T.reshape(heads, DH, D).transpose(1, 0, 2).reshape(DH, heads * D))

    def rows(dyn, shared):
        return lay(np.concatenate([np.asarray(dyn).reshape(-1, D), np.asarray(shared).reshape(-1, D)]).T)

    def down(dyn, shared):
        units = np.concatenate([np.asarray(a).transpose(0, 2, 1).reshape(-1, D) for a in (dyn, shared)])
        return lay(units.reshape(-1, P, D).transpose(1, 0, 2).reshape(P, -1))

    arrays = {
        "x_in": lay(x),
        "ctx_t": lay(ctx.reshape(-1, D).T),
        "wq_t": by_head(L0_xattn_W_q),
        "wk_t": by_head(L0_xattn_W_k),
        "w_v": lay(L0_xattn_W_v),
        "w_o": lay(L0_xattn_W_o),
        "b_o": lay(np.asarray(L0_xattn_b_o).reshape(1, D)),
        "gate_t": lay(np.asarray(L0_ffn_gate_w).T),
        "wg_t": rows(L0_ffn_dyn_gate_w, L0_ffn_sh_gate_w),
        "wu_t": rows(L0_ffn_dyn_up_w, L0_ffn_sh_up_w),
        "wd_t": down(L0_ffn_dyn_down_w, L0_ffn_sh_down_w),
    }
    nc = bacc.Bacc("TRN2", target_bir_lowering=False, num_devices=1)
    aps = [nc.dram_tensor(k, a.shape, F32, kind="ExternalInput").ap() for k, a in arrays.items()]
    out = nc.dram_tensor("out", x.shape, F32, kind="ExternalOutput").ap()
    xattn_moe(nc, *aps, out)
    r = run_bass_kernel_spmd(nc, [arrays], core_ids=[0])
    return r.results[0]["out"]
```

```python
from contextlib import ExitStack

import concourse.bass as bass
from concourse import mybir

F32 = mybir.dt.float32
F32R = mybir.dt.float32r
BF16 = mybir.dt.bfloat16
ALU = mybir.AluOpType
ACT = mybir.ActivationFunctionType
X = mybir.AxisListType.X

P = 128
DH = 64
TOP_K = 4
TOP_P = 0.75
JITTER = 0.2
EPS = 1e-5
HIDE = 1e30



def xattn_moe(nc, x, ctx_t, wq_t, wk_t, w_v, w_o, b_o, gate_t, wg_t, wu_t, wd_t, out):
    B = x.shape[0]
    T = B * P
    H = wq_t.shape[1] // P
    PAIRS = B // 2
    GROUPS = H // 4
    UNITS = 2 * GROUPS
    E = gate_t.shape[1]
    ED = E - 1
    FC = wd_t.shape[1] // P
    CAP = max(-(-T * 5 // (4 * ED)), 4)
    TB = 4
    FG = B // TB
    HALF = H // 2 * P
    WPIECE = FC * P // 3
    WARM = 8
    W3 = 32
    W3K = 3 * W3
    FIRST_CHUNK = 3
    BESIDE = 2 * UNITS - FIRST_CHUNK
    assert UNITS == 8 and FC == 6 and B % 4 == 0

    def on(q):
        return 0 <= q < PAIRS if isinstance(q, int) else True

    def at(p, first):
        return isinstance(p, int) and p == first

    def shift(p, j, d):
        t = j + d
        return p + t // UNITS, t % UNITS

    def wait(eng, sem, value):
        if not isinstance(value, int) or value > 0:
            eng.wait_ge(sem, value)

    def many(value, most):
        return max(0, min(most, value)) if isinstance(value, int) else value

    def chunk_beside(p, j):
        n = UNITS * (p - PAIRS) + j - FIRST_CHUNK if isinstance(p, int) else -1
        return n if n >= 0 else None

    def cols(q, n):
        return bass.ds(q * n, n)

    with ExitStack() as ctx:
        def sb(name, shape, dt=F32):
            return ctx.enter_context(nc.sbuf_tensor(name, shape, dt))

        def psum(name, shape):
            return ctx.enter_context(nc.psum_tensor(name, shape, F32))

        def sem(name):
            return ctx.enter_context(nc.semaphore(name))

        x_all = sb("x_all", [P, B, P])
        ctx_all = sb("ctx_all", [P, T])
        wq = sb("wq", [DH, H * P])
        wk = sb("wk", [DH, H * P])
        wv = sb("wv", [P, H * DH])
        wo = sb("wo", [P, H // 2, P])
        bo = sb("bo", [P, P])
        gate = sb("gate", [P, E])
        wg = sb("wg", [P, FC * P])
        wu = sb("wu", [P, FC * P])
        wd = sb("wd", [P, FC, P])
        ctx_hi = sb("ctx_hi", [P, T], F32R)
        ctx_lo = sb("ctx_lo", [P, T], F32R)
        ctxv_hi = sb("ctxv_hi", [P, 2 * P], F32R)
        ctxv_lo = sb("ctxv_lo", [P, 2 * P], F32R)
        a_hi = sb("a_hi", [P, H, P], F32R)
        a_lo = sb("a_lo", [P, H, P], F32R)
        wv_hi = sb("wv_hi", [P, H * DH], F32R)
        wv_lo = sb("wv_lo", [P, H * DH], F32R)
        wg_hi = sb("wg_hi", [P, FC * P], F32R)
        wg_lo = sb("wg_lo", [P, FC * P], F32R)
        wu_hi = sb("wu_hi", [P, FC * P], F32R)
        wu_lo = sb("wu_lo", [P, FC * P], F32R)
        z_hi = sb("z_hi", [P, 2, 4, 2, P], F32R)
        z_lo = sb("z_lo", [P, 2, 4, 2, P], F32R)
        xt_hi = sb("xt_hi", [P, 2, P], F32R)
        xt_lo = sb("xt_lo", [P, 2, P], F32R)
        x2_hi = sb("x2_hi", [P, T], F32R)
        x2_lo = sb("x2_lo", [P, T], F32R)
        stat1 = sb("stat1", [P, 2, 6])
        mv1 = sb("mv1", [P, 2, 2])
        var1 = sb("var1", [P, 2])
        rstd1 = sb("rstd1", [P, 2])
        xn = sb("xn", [P, 2, P])
        xt = sb("xt", [P, 2 * P])
        neg_max = sb("neg_max", [P, 2, 4])
        row_sum = sb("row_sum", [P, 2, 4])
        row_inv = sb("row_inv", [P, 2, 4])
        prob = sb("prob", [P, 2, 4, P])
        prob_n = sb("prob_n", [P, 2, 4, P])
        prob_t = sb("prob_t", [P, 2, 4, P])
        v = sb("v", [P, 2, H * DH])
        ot = sb("ot", [P, 2, 2, P])
        xb = sb("xb", [P, 2, P])
        x1 = sb("x1", [P, 2, P])
        x1_all = sb("x1_all", [P, T])
        stat2 = sb("stat2", [P, 2, 6])
        mv2 = sb("mv2", [P, 2, 2])
        var2 = sb("var2", [P, 2])
        rstd2 = sb("rstd2", [P, 2])
        x2n = sb("x2n", [P, 2, P])
        x2t = sb("x2t", [P, 2 * P])
        logit = sb("logit", [P, 2, E])
        size = sb("size", [P, 2, ED])
        gap = sb("gap", [P, 2, ED, ED])
        big = sb("big", [P, 2, ED, ED])
        keep = sb("keep", [P, 2, ED, ED])
        tie = sb("tie", [P, 2, ED, ED])
        ahead = sb("ahead", [P, 2, ED, ED])
        gap0 = sb("gap0", [P, 2, ED, ED])
        near = sb("near", [P, 2, ED, ED])
        e_gap = sb("e_gap", [P, 2, ED, ED])
        e_near = sb("e_near", [P, 2, ED, ED])
        e_ahead = sb("e_ahead", [P, 2, ED, ED])
        denom = sb("denom", [P, 2, ED])
        rank = sb("rank", [P, 2, ED])
        top = sb("top", [P, 2])
        below = sb("below", [P, 2, ED])
        e_dyn = sb("e_dyn", [P, 2, ED])
        mass = sb("mass", [P, 2, ED])
        total = sb("total", [P, 2])
        small = sb("small", [P, 2, ED])
        valid = sb("valid", [P, 2, ED])
        mult = sb("mult", [P, 2, ED])
        mult_v = sb("mult_v", [P, 2, ED])
        mult_sum = sb("mult_sum", [P, 2])
        mult_inv = sb("mult_inv", [P, 2])
        rw = sb("rw", [P, 2, ED])
        taken = sb("taken", [P, 2, ED], BF16)
        carry = sb("carry", [P, 3, ED], BF16)
        count = sb("count", [P, 2, ED])
        fits = sb("fits", [P, 2, ED])
        shown = sb("shown", [P, 2, ED])
        hidden = sb("hidden", [P, 2, ED])
        masked = sb("masked", [P, 2, E])
        top2 = sb("top2", [P, 2])
        below2 = sb("below2", [P, 2, E])
        e_all = sb("e_all", [P, 2, E])
        total2 = sb("total2", [P, 2])
        total_dyn = sb("total_dyn", [P, 2])
        inv2 = sb("inv2", [P, 2])
        share_dyn = sb("share_dyn", [P, 2])
        gd = sb("gd", [P, 2, ED])
        w = sb("w", [P, 2, E])
        w_rest = sb("w_rest", [P, 2, E])
        w3 = sb("w3", [P, 2, W3K], BF16)
        w3_all = sb("w3_all", [W3K, T], BF16)
        act = sb("act", [P, 2, TB * P])
        gu = sb("gu", [P, 2, TB * P])
        hid = sb("hid", [P, 3, TB * P])
        y = sb("y", [P, 2, TB * P])
        ident = sb("ident", [P, P])
        ident_b = sb("ident_b", [P, P], BF16)
        upto = sb("upto", [P, P], BF16)
        ones = sb("ones", [P, P], BF16)
        first = sb("first", [P, 2, ED, ED])
        pick = sb("pick", [W3K, FC - 1, P], BF16)
        warm = sb("warm", [P, 512], BF16)
        power = sb("power", [P, 2])
        eps = sb("eps", [P, 2])

        z_ps = psum("z_ps", [P, 2, 512])
        s_ps = psum("s_ps", [P, 2, 512])
        t_ps = psum("t_ps", [P, 512])
        o_ps = psum("o_ps", [P, 512])
        acc_ps = psum("acc_ps", [P, 512])
        v_ps = psum("v_ps", [P, 512])
        aux = o_ps[:, 256:512]
        aux_b = aux.bitcast(BF16)

        d_wk0, d_wq0, d_wk, d_wq, d_ctx0, d_ctx, d_x0, d_x, d_wv, d_wo, d_bo, d_gate, d_wg, d_wu, d_wd = (
            sem("d_" + n) for n in "wk0 wq0 wk wq ctx0 ctx x0 x wv wo bo gate wg wu wd".split())
        zeroed, made, warm_ready = sem("zeroed"), sem("made"), sem("warm_ready")
        ctx_split = sem("ctx_split")
        a_mm, a_hi_done, a_lo_done = sem("a_mm"), sem("a_hi_done"), sem("a_lo_done")
        wv_split = sem("wv_split")
        w_split = sem("w_split")
        ctxv_ready = sem("ctxv_ready")
        ln1, ln1_rstd, xn_ready, xt_mm, xt_ready, xt_split = (
            sem(n) for n in "ln1 ln1_rstd xn_ready xt_mm xt_ready xt_split".split())
        z_mm, z_hi_done, z_lo_done = sem("z_mm"), sem("z_hi_done"), sem("z_lo_done")
        s_done, max_done, exp_done, inv_done, norm_done = (
            sem(n) for n in "s_done max_done exp_done inv_done norm_done".split())
        t_done, pt_done, av_done, ot_done, wo_done = (
            sem(n) for n in "t_done pt_done av_done ot_done wo_done".split())
        v_mm, v_ready = sem("v_mm"), sem("v_ready")
        xb_ready, x1_done, x1_kept = sem("xb_ready"), sem("x1_done"), sem("x1_kept")
        ln2, ln2_rstd, x2n_ready, x2_mm, x2t_ready, x2_split = (
            sem(n) for n in "ln2 ln2_rstd x2n_ready x2_mm x2t_ready x2_split".split())
        logit_mm, logit_ready = sem("logit_mm"), sem("logit_ready")
        step, router_exp = sem("step"), sem("router_exp")
        count_mm, count_ready = sem("count_mm"), sem("count_ready")
        w3_mm, w3_ready = sem("w3_mm"), sem("w3_ready")
        g_mm, u_mm, wb_mm, silu_done, gu_done, hid_done, down_done, y_done = (
            sem(n) for n in "g_mm u_mm wb_mm silu_done gu_done hid_done down_done y_done".split())
        stored = [sem(f"stored{k}") for k in range(2)]

        GAPS, CHOICES, FITTING, WEIGHTS = 5, 23, 34, 46

        with nc.Block() as block:
            @block.sync
            def _(sp):
                x_v = x.rearrange("b t d -> t b d")
                sp.dma_start(wk[:, 0:HALF], wk_t[:, 0:HALF]).then_inc(d_wk0, 16)
                sp.dma_start(ctx_all[:, 0:2 * P], ctx_t[:, 0:2 * P]).then_inc(d_ctx0, 16)
                sp.dma_start(wk[:, HALF:], wk_t[:, HALF:]).then_inc(d_wk, 16)
                sp.dma_start(wv[:], w_v).then_inc(d_wv, 16)
                sp.dma_start(ctx_all[:, 2 * P:T], ctx_t[:, 2 * P:T]).then_inc(d_ctx, 16)
                sp.dma_start(x_all[:, 2:B, :], x_v[:, 2:B, :]).then_inc(d_x, 16)
                sp.dma_start(wo[:], w_o.rearrange("(c p) d -> p c d", p=P)).then_inc(d_wo, 16)
                sp.dma_start(wg[:], wg_t).then_inc(d_wg, 16)
                sp.dma_start(wu[:], wu_t).then_inc(d_wu, 16)
                sp.dma_start(wd[:].rearrange("p c d -> p (c d)"), wd_t).then_inc(d_wd, 16)
                out_v = out.rearrange("b t d -> t b d")
                for g in range(FG):
                    sp.wait_ge(y_done, g + 1)
                    sp.dma_start(out_v[:, TB * g:TB * g + TB, :],
                                 y[:, g % 2, :].rearrange("p (b d) -> p b d", b=TB)).then_inc(stored[g % 2], 16)
                for k in range(2):
                    sp.wait_ge(stored[k], 16 * (FG // 2))

            @block.gpsimd
            def _(pool):
                nc.gpsimd.memset(warm[:], 0.0).then_inc(warm_ready, 1)
                nc.gpsimd.memset(ident[:], 0.0).then_inc(zeroed, 1)
                nc.gpsimd.memset(power[:], -0.5).then_inc(zeroed, 1)
                nc.gpsimd.memset(eps[:], EPS).then_inc(zeroed, 1)
                pool.wait_ge(zeroed, 3)
                nc.gpsimd.affine_select(out=ident[:], in_=ident[:], compare_op=ALU.not_equal, fill=1.0, base=0,
                                        pattern=[[-1, P]], channel_multiplier=1).then_inc(made, 1)
                nc.gpsimd.memset(ident_b[:], 0.0).then_inc(zeroed, 1)
                nc.gpsimd.memset(upto[:], 0.0).then_inc(zeroed, 1)
                nc.gpsimd.memset(first[:], 0.0).then_inc(zeroed, 1)
                nc.gpsimd.memset(pick[:], 0.0).then_inc(zeroed, 1)
                nc.gpsimd.memset(w3[:], 0.0).then_inc(zeroed, 1)
                nc.gpsimd.memset(carry[:], 0.0).then_inc(zeroed, 1)
                nc.gpsimd.memset(ones[:], 1.0).then_inc(zeroed, 1)

                def router_constants():
                    pool.wait_ge(zeroed, 10)
                    nc.gpsimd.affine_select(out=ident_b[:], in_=ident_b[:], compare_op=ALU.not_equal, fill=1.0,
                                            base=0, pattern=[[-1, P]], channel_multiplier=1).then_inc(made, 1)
                    nc.gpsimd.affine_select(out=upto[:], in_=upto[:], compare_op=ALU.is_gt, fill=1.0, base=0,
                                            pattern=[[-1, P]], channel_multiplier=1).then_inc(made, 1)
                    nc.gpsimd.affine_select(out=first[:], in_=first[:], compare_op=ALU.is_ge, fill=1.0, base=0,
                                            pattern=[[0, 2], [-1, ED], [1, ED]], channel_multiplier=0).then_inc(made, 1)

                    for part in range(3):
                        pool.wait_ge(made, 4 + 2 * part)
                        rows = pick[W3 * part:W3 * part + W3]
                        dyn = rows[:, 0:ED // 2, :].rearrange("r c (h i) -> r c h i", h=2)
                        nc.gpsimd.affine_select(out=dyn, in_=dyn, compare_op=ALU.not_equal, fill=1.0, base=0,
                                                pattern=[[-2, ED // 2], [-1, 2], [0, DH]],
                                                channel_multiplier=1).then_inc(made, 1)
                        shared = rows[:, ED // 2, :]
                        nc.gpsimd.affine_select(out=shared, in_=shared, compare_op=ALU.not_equal, fill=1.0,
                                                base=-ED, pattern=[[0, P]], channel_multiplier=1).then_inc(made, 1)
                    pool.wait_ge(made, 10)

                def split_weights(src, hi, lo, landed, n, piece):
                    unit = cols(piece, WPIECE)
                    pool.wait_ge(landed, 16)
                    nc.gpsimd.tensor_copy(hi[:, unit], src[:, unit]).then_inc(w_split, 1)
                    pool.wait_ge(w_split, n + 1)
                    nc.gpsimd.tensor_tensor(lo[:, unit], src[:, unit], hi[:, unit].bitcast(F32),
                                            ALU.subtract).then_inc(w_split, 1)

                def slot(p, j):
                    if j == 2 and on(p + 1):
                        q = p + 1
                        wait(pool, ln1, 4 * q + 4)
                        nc.gpsimd.tensor_tensor(var1[:], mv1[:, :, 1], eps[:], ALU.add).then_inc(ln1_rstd, 1)
                        wait(pool, ln1_rstd, 2 * q + 1)
                        nc.gpsimd.tensor_tensor(rstd1[:], var1[:], power[:], ALU.pow).then_inc(ln1_rstd, 1)
                    if j == 5 and on(p - 1):
                        q = p - 1
                        wait(pool, ln2, 4 * q + 4)
                        nc.gpsimd.tensor_tensor(var2[:], mv2[:, :, 1], eps[:], ALU.add).then_inc(ln2_rstd, 1)
                        wait(pool, ln2_rstd, 2 * q + 1)
                        nc.gpsimd.tensor_tensor(rstd2[:], var2[:], power[:], ALU.pow).then_inc(ln2_rstd, 1)
                    q, u = shift(p, j, -1)
                    if on(q):
                        n = UNITS * q + u
                        wait(pool, inv_done, n + 1)
                        wait(pool, t_done, n - 1)
                        nc.gpsimd.tensor_tensor(prob_n[:, u % 2], prob[:, u % 2],
                                                row_inv[:, u % 2, :].unsqueeze(2).to_broadcast([P, 4, P]),
                                                ALU.mult).then_inc(norm_done, 1)
                    if j == 6 and on(p):
                        if at(p, 0):
                            pool.wait_ge(d_bo, 16)
                            pool.wait_ge(d_x0, 16)
                            pool.wait_ge(d_x, 16)
                        wait(pool, x1_done, p)
                        nc.gpsimd.tensor_tensor(xb[:], x_all[:, cols(p, 2), :],
                                                bo[:].unsqueeze(1).to_broadcast([P, 2, P]),
                                                ALU.add).then_inc(xb_ready, 1)
                    if j == 5 and on(p + 1):
                        q = p + 1
                        if at(q, 0):
                            pool.wait_ge(ctx_split, 2)
                        if at(q, 1):
                            pool.wait_ge(ctx_split, 4)
                        if at(q, 2):
                            pool.wait_ge(ctx_split, 10)
                        wait(pool, v_mm, 4 * q)
                        nc.gpsimd.tensor_copy(ctxv_hi[:], ctx_hi[:, cols(q, 2 * P)]).then_inc(ctxv_ready, 1)
                        nc.gpsimd.tensor_copy(ctxv_lo[:], ctx_lo[:, cols(q, 2 * P)]).then_inc(ctxv_ready, 1)
                    if j == 4 and on(p - 1):
                        wait(pool, x1_done, p)
                        nc.gpsimd.tensor_copy(x1_all[:, cols(p - 1, 2 * P)],
                                              x1[:].rearrange("p b d -> p (b d)")).then_inc(x1_kept, 1)
                    if j == 7 and on(p - 1):
                        q = p - 1
                        wait(pool, x2t_ready, q + 1)
                        nc.gpsimd.tensor_copy(x2_hi[:, cols(q, 2 * P)], x2t[:]).then_inc(x2_split, 1)
                        wait(pool, x2_split, 2 * q + 1)
                        nc.gpsimd.tensor_tensor(x2_lo[:, cols(q, 2 * P)], x2t[:],
                                                x2_hi[:, cols(q, 2 * P)].bitcast(F32),
                                                ALU.subtract).then_inc(x2_split, 1)
                    if at(p, -1) and j == 5:
                        pool.wait_ge(d_wv, 16)
                        pool.wait_ge(wv_split, 1)
                        nc.gpsimd.tensor_tensor(wv_lo[:], wv[:], wv_hi[:].bitcast(F32),
                                                ALU.subtract).then_inc(wv_split, 1)
                    if at(p, -1) and j == 7:
                        router_constants()
                    if at(p, 0) and j in (1, 4, 7):
                        piece = (1, 4, 7).index(j)
                        split_weights(wg, wg_hi, wg_lo, d_wg, 2 * piece, piece)
                    if at(p, 1) and j in (0, 1, 3):
                        piece = (0, 1, 3).index(j)
                        split_weights(wu, wu_hi, wu_lo, d_wu, 6 + 2 * piece, piece)

                for p in (-1, 0, 1):
                    for j in range(UNITS):
                        slot(p, j)
                with pool.Fori(2, PAIRS - 1) as p:
                    for j in range(UNITS):
                        slot(p, j)
                for p in (PAIRS - 1, PAIRS, PAIRS + 1):
                    for j in range(UNITS):
                        slot(p, j)

            @block.scalar
            def _(sc):
                sc.dma_start(wq[:, 0:HALF], wq_t[:, 0:HALF]).then_inc(d_wq0, 16)
                sc.dma_start(x_all[:, 0:2, :], x.rearrange("b t d -> t b d")[:, 0:2, :]).then_inc(d_x0, 16)
                sc.dma_start(wq[:, HALF:], wq_t[:, HALF:]).then_inc(d_wq, 16)
                sc.dma_start(bo[:], b_o.to_broadcast([P, P])).then_inc(d_bo, 16)
                sc.dma_start(gate[:], gate_t).then_inc(d_gate, 16)
                for g in range(GROUPS):
                    sc.wait_ge(a_mm, g + 1)
                    bank = (z_ps, s_ps)[g // 2][:, g % 2, :]
                    nc.scalar.activation(a_hi[:, 4 * g:4 * g + 4, :].rearrange("p h d -> p (h d)"), bank, ACT.Copy,
                                         scale=DH ** -0.5).then_inc(a_hi_done, 1)
                sc.wait_ge(d_wv, 16)
                nc.scalar.activation(wv_hi[:], wv[:], ACT.Copy).then_inc(wv_split, 1)

                def chunk(n):
                    c = n % FC
                    sc.wait_ge(g_mm, n + 1)
                    wait(sc, gu_done, n - 1)
                    nc.scalar.activation(act[:, c % 2, :], z_ps[:, c % 2, :], ACT.Silu).then_inc(silu_done, 1)

                def slot(p, j):
                    if chunk_beside(p, j) is not None:
                        chunk(chunk_beside(p, j))
                    if j == 1 and on(p - 2):
                        wait(sc, step, WEIGHTS * (p - 2) + GAPS)
                        nc.scalar.activation(e_gap[:], gap0[:], ACT.Exp, scale=-1.0).then_inc(router_exp, 1)
                        nc.scalar.activation(e_dyn[:], below[:], ACT.Exp).then_inc(router_exp, 1)
                    q, z = shift(p, j, 3)
                    if on(q):
                        wait(sc, z_mm, UNITS * q + z + 1)
                        wait(sc, s_done, UNITS * q + 2 * (z // 2) - 2)
                        nc.scalar.activation(
                            z_hi[:, (z // 2) % 2, 2 * (z % 2):2 * (z % 2) + 2].rearrange("p h b m -> p (h b m)"),
                            z_ps[:, z % 2, :], ACT.Copy).then_inc(z_hi_done, 1)
                    if on(p):
                        n = UNITS * p + j
                        wait(sc, max_done, n + 1)
                        wait(sc, norm_done, n - 1)
                        for h in range(4):
                            last = nc.scalar.activation(
                                prob[:, j % 2, h, :], s_ps[:, j % 2, h * P:(h + 1) * P], ACT.Exp,
                                bias=neg_max[:, j % 2, h:h + 1], accum_out=row_sum[:, j % 2, h:h + 1])
                        last.then_inc(exp_done, 1)
                    if j == 5 and on(p - 2):
                        wait(sc, step, WEIGHTS * (p - 2) + FITTING)
                        nc.scalar.activation(e_all[:], below2[:], ACT.Exp).then_inc(router_exp, 1)
                    q, u = shift(p, j, -2)
                    if on(q) and u % 2:
                        n = UNITS * q + u
                        wait(sc, t_done, n + 1)
                        wait(sc, av_done, n - 1)
                        nc.scalar.activation(prob_t[:, 1].rearrange("p h t -> p (h t)"), t_ps[:],
                                             ACT.Copy).then_inc(pt_done, 1)
                    q, u = shift(p, j, -3)
                    if on(q):
                        wait(sc, av_done, UNITS * q + u + 1)
                    if j == 3 and on(p - 2):
                        wait(sc, count_mm, p - 1)
                        nc.scalar.activation(count[:].rearrange("p b e -> p (b e)"), aux[:, 0:2 * ED],
                                             ACT.Copy).then_inc(count_ready, 1)
                    if j == 5 and on(p + 1):
                        wait(sc, xt_mm, p + 2)
                        wait(sc, xt_split, 4 * (p + 1))
                        nc.scalar.activation(xt[:], aux, ACT.Copy).then_inc(xt_ready, 1)
                    if j == 6 and on(p - 1):
                        wait(sc, x2_mm, p)
                        wait(sc, x2_split, 2 * (p - 1))
                        wait(sc, logit_mm, p - 1)
                        nc.scalar.activation(x2t[:], aux, ACT.Copy).then_inc(x2t_ready, 1)
                    if j == 7 and on(p - 1):
                        wait(sc, logit_mm, p)
                        wait(sc, step, WEIGHTS * (p - 1))
                        nc.scalar.activation(logit[:].rearrange("p b e -> p (b e)"), aux[:, 0:2 * E],
                                             ACT.Copy).then_inc(logit_ready, 1)
                    if j == 7 and on(p - 2):
                        wait(sc, w3_mm, p - 1)
                        nc.scalar.activation(w3_all[:, cols(p - 2, 2 * P)], aux_b[0:W3K, P:P + 2 * P],
                                             ACT.Copy).then_inc(w3_ready, 1)
                    if on(q):
                        n = UNITS * q + u
                        wait(sc, wo_done, n - 1)
                        nc.scalar.activation(ot[:, u % 2].rearrange("p c t -> p (c t)"), o_ps[:, 0:256],
                                             ACT.Copy).then_inc(ot_done, 1)
                    q, vi = {7: (p + 1, 0), 0: (p, 1), 3: (p, 2), 4: (p, 3)}.get(j, (PAIRS, 0))
                    if on(q):
                        wait(sc, v_mm, 4 * q + vi + 1)
                        wait(sc, av_done, UNITS * (q - 1) + (2, 3, 6, 7)[vi] + 1)
                        nc.scalar.activation(v[:, vi % 2, (vi // 2) * 512:(vi // 2) * 512 + 512], v_ps[:],
                                             ACT.Copy).then_inc(v_ready, 1)

                for p in (-1, 0, 1):
                    for j in range(UNITS):
                        slot(p, j)
                with sc.Fori(2, PAIRS - 1) as p:
                    for j in range(UNITS):
                        slot(p, j)
                for p in (PAIRS - 1, PAIRS, PAIRS + 1):
                    for j in range(UNITS):
                        slot(p, j)

                for n in range(BESIDE, FC * FG):
                    chunk(n)

            @block.vector
            def _(ve):
                def a_low(g):
                    ve.wait_ge(a_hi_done, g + 1)
                    bank = (z_ps, s_ps)[g // 2][:, g % 2, :]
                    nc.vector.scalar_tensor_tensor(
                        a_lo[:, 4 * g:4 * g + 4, :].rearrange("p h d -> p (h d)"), bank, DH ** -0.5,
                        a_hi[:, 4 * g:4 * g + 4, :].rearrange("p h d -> p (h d)").bitcast(F32),
                        ALU.mult, ALU.subtract).then_inc(a_lo_done, 1)

                def split_ctx(start, end, n):
                    nc.vector.tensor_copy(ctx_hi[:, start:end], ctx_all[:, start:end]).then_inc(ctx_split, 1)
                    ve.wait_ge(ctx_split, n + 1)
                    nc.vector.tensor_tensor(ctx_lo[:, start:end], ctx_all[:, start:end],
                                            ctx_hi[:, start:end].bitcast(F32), ALU.subtract).then_inc(ctx_split, 1)

                ve.wait_ge(d_ctx0, 16)
                split_ctx(0, 2 * P, 0)

                class Steps:

                    def __init__(self, q):
                        self.before, self.n = WEIGHTS * q, 0

                    def done(self, ins):
                        self.n += 1
                        ins.then_inc(step, 1)

                    def wait_all(self):
                        wait(ve, step, self.before + self.n)

                def flat(a):
                    return a[:].rearrange("p b j i -> p (b j i)")

                def wide(a, n=ED):
                    return a[:].unsqueeze(2).to_broadcast([P, 2, n])

                def of_j(a):
                    return a.unsqueeze(3).to_broadcast([P, 2, ED, ED])

                def of_i(a):
                    return a.unsqueeze(2).to_broadcast([P, 2, ED, ED])

                tensor, two, scale, red = (nc.vector.tensor_tensor, nc.vector.scalar_tensor_tensor,
                                           nc.vector.tensor_scalar, nc.vector.tensor_reduce)
                s = logit[:, :, 0:ED]

                def router(q, r, j, place):
                    at_place = (j, place)
                    if at_place == (0, 0):
                        wait(ve, logit_ready, q + 1)
                        r.done(tensor(gap[:], of_j(s), of_i(s), ALU.subtract))
                        r.done(two(size[:], s, -1.0, s, ALU.mult, ALU.max))
                        r.done(red(top[:], s, X, ALU.max))
                    if at_place == (0, 1):
                        r.wait_all()
                        r.done(scale(flat(gap0), flat(gap), 0.0, None, ALU.max))
                        r.done(tensor(below[:], s, wide(top), ALU.subtract))
                        assert r.n == GAPS
                    if at_place == (0, 2):
                        r.wait_all()
                        r.done(tensor(big[:], of_j(size[:]), of_i(size[:]), ALU.max))
                        r.done(two(flat(tie), flat(gap), 0.0, flat(first), ALU.is_equal, ALU.mult))
                    if at_place == (0, 3):
                        r.wait_all()
                        r.done(two(flat(ahead), flat(gap), 0.0, flat(tie), ALU.is_lt, ALU.add))
                        r.done(two(flat(keep), flat(big), JITTER, flat(gap), ALU.mult, ALU.is_ge))
                    if at_place == (1, 0):
                        r.wait_all()
                        r.done(two(flat(near), flat(ahead), 0.5, flat(keep), ALU.is_lt, ALU.mult))
                    if at_place == (1, 3):
                        r.wait_all()
                        wait(ve, router_exp, 3 * q + 2)
                        r.done(tensor(flat(e_near), flat(e_gap), flat(near), ALU.mult))
                        r.done(red(rank[:], ahead[:], X, ALU.add))
                        r.done(red(total[:], e_dyn[:], X, ALU.add))
                        r.done(tensor(e_ahead[:], ahead[:], of_i(e_dyn[:]), ALU.mult))
                    if at_place == (2, 0):
                        r.wait_all()
                        r.done(red(denom[:], e_near[:], X, ALU.add))
                        r.done(red(mass[:], e_ahead[:], X, ALU.add))
                    if at_place == (2, 1):
                        r.wait_all()
                        r.done(nc.vector.reciprocal(mult[:], denom[:]))
                        r.done(two(small[:], wide(total), TOP_P, mass[:], ALU.mult, ALU.is_gt))
                    if at_place == (2, 2):
                        r.wait_all()
                        r.done(two(valid[:], rank[:], float(TOP_K), small[:], ALU.is_lt, ALU.mult))
                    if at_place == (2, 3):
                        r.wait_all()
                        r.done(nc.vector.tensor_copy(taken[:], valid[:]))
                        r.done(tensor(mult_v[:], mult[:], valid[:], ALU.mult))
                        r.done(nc.vector.tensor_copy(carry[:, 0, :], carry[:, 2, :]))
                    if at_place == (3, 0):
                        r.wait_all()
                        r.done(tensor(carry[:, 1, :], carry[:, 0, :], taken[:, 0, :], ALU.add))
                        assert r.n == CHOICES
                    if at_place == (3, 1):
                        r.wait_all()
                        r.done(tensor(carry[:, 2, :], carry[:, 1, :], taken[:, 1, :], ALU.add))
                        r.done(red(mult_sum[:], mult_v[:], X, ALU.add))
                    if at_place == (4, 1):
                        r.wait_all()
                        wait(ve, count_ready, q + 1)
                        r.done(two(fits[:], count[:], float(CAP), valid[:], ALU.is_le, ALU.mult))
                    if at_place == (4, 2):
                        r.wait_all()
                        r.done(tensor(shown[:], s, fits[:], ALU.mult))
                        r.done(scale(hidden[:], fits[:], 1.0, HIDE, ALU.subtract, ALU.mult))
                        r.done(nc.vector.tensor_copy(masked[:, :, ED:E], logit[:, :, ED:E]))
                        r.done(nc.vector.reciprocal(mult_inv[:], mult_sum[:]))
                    if at_place == (4, 3):
                        r.wait_all()
                        r.done(tensor(masked[:, :, 0:ED], shown[:], hidden[:], ALU.add))
                        r.done(tensor(rw[:], mult_v[:], wide(mult_inv), ALU.mult))
                    if at_place == (5, 0):
                        r.wait_all()
                        r.done(red(top2[:], masked[:], X, ALU.max))
                    if at_place == (5, 1):
                        r.wait_all()
                        r.done(tensor(below2[:], masked[:], wide(top2, E), ALU.subtract))
                        assert r.n == FITTING
                    if at_place == (5, 3):
                        r.wait_all()
                        wait(ve, router_exp, 3 * q + 3)
                        r.done(red(total2[:], e_all[:], X, ALU.add))
                        r.done(red(total_dyn[:], e_all[:, :, 0:ED], X, ALU.add))
                    if at_place == (6, 0):
                        r.wait_all()
                        r.done(nc.vector.reciprocal(inv2[:], total2[:]))
                    if at_place == (6, 1):
                        r.wait_all()
                        if isinstance(q, int):
                            wait(ve, w3_mm, q)
                        r.done(tensor(share_dyn[:], total_dyn[:], inv2[:], ALU.mult))
                        r.done(tensor(w[:, :, ED:E], e_all[:, :, ED:E], wide(inv2, 1), ALU.mult))
                        r.done(tensor(w3[:, :, ED:E], e_all[:, :, ED:E], wide(inv2, 1), ALU.mult))
                    if at_place == (6, 2):
                        r.wait_all()
                        r.done(tensor(gd[:], rw[:], wide(share_dyn), ALU.mult))
                        r.wait_all()
                        r.done(tensor(w[:, :, 0:ED], gd[:], fits[:], ALU.mult))
                        r.done(tensor(w3[:, :, 0:ED], gd[:], fits[:], ALU.mult))
                    if at_place == (6, 3):
                        r.wait_all()
                        r.done(tensor(w_rest[:], w[:], w3[:, :, 0:E], ALU.subtract))
                    if at_place == (7, 0):
                        r.wait_all()
                        r.done(nc.vector.tensor_copy(w3[:, :, W3:W3 + E], w_rest[:]))
                        r.wait_all()
                        r.done(tensor(w3[:, :, 2 * W3:2 * W3 + E], w_rest[:], w3[:, :, W3:W3 + E], ALU.subtract))
                        assert r.n == WEIGHTS

                def residual(g):
                    wait(ve, down_done, FC * g + FC)
                    wait(ve, stored[g % 2], 16 * (g // 2))
                    nc.vector.tensor_tensor(y[:, g % 2, :], acc_ps[:], x1_all[:, cols(g, TB * P)],
                                            ALU.add).then_inc(y_done, 1)

                def chunk(n):
                    g, c = n // FC, n % FC
                    ve.wait_ge(silu_done, n + 1)
                    ve.wait_ge(u_mm, n + 1)
                    nc.vector.tensor_tensor(gu[:, c % 2, :], s_ps[:, c % 2, :], act[:, c % 2, :],
                                            ALU.mult).then_inc(gu_done, 1)
                    ve.wait_ge(wb_mm, n + 1)
                    ve.wait_ge(gu_done, n + 1)
                    wait(ve, down_done, n - 2)
                    nc.vector.tensor_tensor(hid[:, c % 3, :], (t_ps if c % 2 else v_ps)[:], gu[:, c % 2, :],
                                            ALU.mult).then_inc(hid_done, 1)
                    if c == 1 and g > 0:
                        residual(g - 1)

                def slot(p, j, r):
                    def route(place):
                        if on(p - 2):
                            router(p - 2, r, j, place)

                    if j == 1 and on(p + 1):
                        q = p + 1
                        if at(q, 0):
                            ve.wait_ge(d_x0, 16)
                        if at(q, 1):
                            ve.wait_ge(d_x, 16)
                        for b in range(2):
                            nc.vector.bn_stats(stat1[:, b, :], x_all[:, cols(2 * q + b, 1), :]
                                               .rearrange("p b d -> p (b d)")).then_inc(ln1, 1)
                        wait(ve, ln1, 4 * q + 2)
                        wait(ve, ln1_rstd, 2 * q)
                    qx, b = (p + 1, 0) if j == 7 else (p, 1)
                    if j in (7, 0) and on(qx):
                        wait(ve, xt_ready, qx + 1)
                        wait(ve, s_done, UNITS * qx - 1 + b)
                        nc.vector.tensor_copy(xt_hi[:, b, :], xt[:, b * P:(b + 1) * P]).then_inc(xt_split, 1)
                    q, u = shift(p, j, -1)
                    if on(q):
                        wait(ve, exp_done, UNITS * q + u + 1)
                        nc.vector.reciprocal(row_inv[:, u % 2, :], row_sum[:, u % 2, :]).then_inc(inv_done, 1)
                    if at(p, 2) and j == 0:
                        ve.wait_ge(made, 10)
                    route(0)
                    if on(p):
                        wait(ve, s_done, UNITS * p + j + 1)
                        nc.vector.tensor_reduce(neg_max[:, j % 2, :],
                                                s_ps[:, j % 2, :].rearrange("p (h m) -> p h m", h=4),
                                                X, ALU.max, negate=True).then_inc(max_done, 1)
                    if j in (7, 0) and on(qx):
                        wait(ve, xt_split, 4 * qx + 2 * b + 1)
                        nc.vector.tensor_tensor(xt_lo[:, b, :], xt[:, b * P:(b + 1) * P],
                                                xt_hi[:, b, :].bitcast(F32), ALU.subtract).then_inc(xt_split, 1)
                    if j == 1 and on(p + 1):
                        for b in range(2):
                            nc.vector.bn_aggr(mv1[:, b, :], stat1[:, b, :]).then_inc(ln1, 1)
                    if j == 3 and on(p + 1):
                        q = p + 1
                        wait(ve, ln1_rstd, 2 * q + 2)
                        wait(ve, xt_mm, q)
                        for b in range(2):
                            nc.vector.tensor_scalar(
                                xn[:, b, :], x_all[:, cols(2 * q + b, 1), :].rearrange("p b d -> p (b d)"),
                                mv1[:, b, 0:1], rstd1[:, b:b + 1], ALU.subtract, ALU.mult).then_inc(xn_ready, 1)
                    if j == 4 and on(p - 1):
                        q = p - 1
                        wait(ve, wo_done, UNITS * q + UNITS)
                        wait(ve, xb_ready, q + 1)
                        wait(ve, x1_kept, q)
                        nc.vector.tensor_tensor(x1[:].rearrange("p b d -> p (b d)"), acc_ps[:, 0:2 * P],
                                                xb[:].rearrange("p b d -> p (b d)"), ALU.add).then_inc(x1_done, 1)
                    if j == 5 and on(p - 1):
                        q = p - 1
                        wait(ve, ln2_rstd, 2 * q + 2)
                        for b in range(2):
                            nc.vector.tensor_scalar(x2n[:, b, :], x1[:, b, :], mv2[:, b, 0:1], rstd2[:, b:b + 1],
                                                    ALU.subtract, ALU.mult).then_inc(x2n_ready, 1)
                    route(1)
                    if j == 4 and on(p - 1):
                        q = p - 1
                        wait(ve, x1_done, q + 1)
                        for b in range(2):
                            nc.vector.bn_stats(stat2[:, b, :], x1[:, b, :]).then_inc(ln2, 1)
                        wait(ve, ln2, 4 * q + 2)
                    if chunk_beside(p, j) is not None:
                        chunk(chunk_beside(p, j))
                    q, u = shift(p, j, -2)
                    if on(q) and u % 2 == 0:
                        n = UNITS * q + u
                        wait(ve, t_done, n + 1)
                        wait(ve, av_done, n - 1)
                        nc.vector.tensor_copy(prob_t[:, 0].rearrange("p h t -> p (h t)"),
                                              t_ps[:]).then_inc(pt_done, 1)
                    if j == 4 and on(p - 1):
                        for b in range(2):
                            nc.vector.bn_aggr(mv2[:, b, :], stat2[:, b, :]).then_inc(ln2, 1)
                    route(2)
                    q, z = shift(p, j, 3)
                    if on(q):
                        wait(ve, z_hi_done, UNITS * q + z + 1)
                        zh = z_hi[:, (z // 2) % 2, 2 * (z % 2):2 * (z % 2) + 2].rearrange("p h b m -> p (h b m)")
                        zl = z_lo[:, (z // 2) % 2, 2 * (z % 2):2 * (z % 2) + 2].rearrange("p h b m -> p (h b m)")
                        nc.vector.tensor_tensor(zl, z_ps[:, z % 2, :], zh.bitcast(F32),
                                                ALU.subtract).then_inc(z_lo_done, 1)
                    route(3)
                    if at(p, -1) and j == 1:
                        a_low(0)
                    if at(p, -1) and j == 3:
                        for g in range(1, GROUPS):
                            a_low(g)
                    if (at(p, 0) or at(p, 1)) and j in (1, 4):
                        piece = 2 * p + (1, 4).index(j)
                        ve.wait_ge(d_ctx, 16)
                        split_ctx(2 * P + 4 * P * piece, min(6 * P + 4 * P * piece, T), 2 + 2 * piece)

                def pair(p):
                    r = Steps(p - 2)
                    for j in range(UNITS):
                        slot(p, j, r)

                for p in (-1, 0, 1):
                    pair(p)
                with ve.Fori(2, PAIRS - 1) as p:
                    pair(p)
                for p in (PAIRS - 1, PAIRS, PAIRS + 1):
                    pair(p)

                for n in range(BESIDE, FC * FG):
                    chunk(n)
                residual(FG - 1)

            @block.tensor
            def _(pe):
                mm = nc.tensor.matmul
                pe.wait_ge(warm_ready, 1)
                for k in range(WARM):
                    mm(acc_ps[:], warm[:, 0:P], warm[:], start=True, stop=True)
                pe.wait_ge(d_wk0, 16)
                pe.wait_ge(d_wq0, 16)
                for g in range(GROUPS):
                    if g == GROUPS // 2:
                        pe.wait_ge(d_wk, 16)
                        pe.wait_ge(d_wq, 16)
                    for h in range(4 * g, 4 * g + 4):
                        bank = (z_ps, s_ps)[g // 2][:, g % 2, :]
                        last = mm(bank[:, (h % 4) * P:(h % 4) * P + P], wk[:, h * P:(h + 1) * P],
                                  wq[:, h * P:(h + 1) * P], start=True, stop=True)
                    last.then_inc(a_mm, 1)

                def split_mm(out, l_hi, l_lo, r_hi, r_lo):
                    mm(out, l_lo, r_hi, start=True, stop=False)
                    mm(out, l_hi, r_lo, start=False, stop=False)
                    return mm(out, l_hi, r_hi, start=False, stop=True)

                LAG = 2

                def project(n):
                    g, c = n // FC, n % FC
                    wait(pe, hid_done, n + 1)
                    if n == 0:
                        pe.wait_ge(d_wd, 16)
                        pe.wait_ge(x1_done, PAIRS)
                    if c == 0:
                        wait(pe, y_done, g)
                    for tile in range(TB):
                        last = mm(acc_ps[:, tile * P:(tile + 1) * P], hid[:, c % 3, tile * P:(tile + 1) * P],
                                  wd[:, c, :], start=(c == 0 and tile == 0), stop=(c == FC - 1),
                                  skip_group_check=True)
                    last.then_inc(down_done, 1)

                def chunk(n):
                    g, c = n // FC, n % FC
                    tok = cols(g, TB * P)
                    unit = slice(c * P, (c + 1) * P)
                    if n == 0:
                        pe.wait_ge(w_split, 12)
                        pe.wait_ge(z_lo_done, UNITS * PAIRS)
                        pe.wait_ge(exp_done, UNITS * PAIRS)
                        pe.wait_ge(v_ready, 4 * PAIRS)
                        pe.wait_ge(pt_done, UNITS * PAIRS)
                    if c == 0:
                        pe.wait_ge(x2_split, TB * (g + 1))
                    wait(pe, silu_done, n - 1)
                    split_mm(z_ps[:, c % 2, :], wg_hi[:, unit], wg_lo[:, unit],
                             x2_hi[:, tok], x2_lo[:, tok]).then_inc(g_mm, 1)
                    wait(pe, gu_done, n - 1)
                    split_mm(s_ps[:, c % 2, :], wu_hi[:, unit], wu_lo[:, unit],
                             x2_hi[:, tok], x2_lo[:, tok]).then_inc(u_mm, 1)
                    if c == 0:
                        pe.wait_ge(w3_ready, TB // 2 * (g + 1))
                    wait(pe, hid_done, n - 1)
                    mm((t_ps if c % 2 else v_ps)[:], pick[:, min(c, ED // 2), :], w3_all[:, tok],
                       start=True, stop=True).then_inc(wb_mm, 1)
                    if n >= LAG:
                        project(n - LAG)

                def slot(p, j):
                    if chunk_beside(p, j) is not None:
                        chunk(chunk_beside(p, j))
                    if on(p):
                        g, b = j // 2, j % 2
                        if at(p, 0) and j < 2:
                            pe.wait_ge(a_lo_done, j + 3)
                        wait(pe, z_lo_done, UNITS * p + 2 * g + 2)
                        wait(pe, xt_split, 4 * p + 2 * b + 2)
                        wait(pe, exp_done, UNITS * p + j - 1)
                        split_mm(s_ps[:, j % 2, :].rearrange("p (h m) -> p h m", h=4), xt_hi[:, b, :], xt_lo[:, b, :],
                                 z_hi[:, g % 2, :, b, :], z_lo[:, g % 2, :, b, :]).then_inc(s_done, 1)
                    q, z = shift(p, j, 3)
                    if on(q):
                        if at(q, 0):
                            pe.wait_ge(a_lo_done, 1 + max(z // 2, z % 2))
                            pe.wait_ge(ctx_split, 2)
                        if at(q, 1) and z == 0:
                            pe.wait_ge(ctx_split, 4)
                        if at(q, 2) and z == 0:
                            pe.wait_ge(ctx_split, 10)
                        wait(pe, z_lo_done, UNITS * q + z - 1)
                        for hh in range(2):
                            h = 2 * z + hh
                            last = split_mm(z_ps[:, z % 2, hh * 256:hh * 256 + 256], a_hi[:, h, :], a_lo[:, h, :],
                                            ctx_hi[:, cols(q, 2 * P)], ctx_lo[:, cols(q, 2 * P)])
                        last.then_inc(z_mm, 1)
                    q, u = shift(p, j, -2)
                    if on(q):
                        n = UNITS * q + u
                        if at(n, 0):
                            pe.wait_ge(made, 1)
                        wait(pe, norm_done, n + 1)
                        wait(pe, pt_done, n)
                        for h in range(4):
                            last = nc.tensor.transpose(t_ps[:, h * P:(h + 1) * P], prob_n[:, u % 2, h, :], ident[:])
                        last.then_inc(t_done, 1)

                    def o_bank_free():
                        wait(pe, ot_done, many(UNITS * p + j - 3, UNITS * PAIRS))
                        if isinstance(p, int):
                            wait(pe, count_ready, many(p - 1 - (j <= 3), PAIRS))
                            wait(pe, xt_ready, many(p + 2 - (j <= 5), PAIRS))
                            wait(pe, x2t_ready, many(p - (j <= 6), PAIRS))
                            wait(pe, logit_ready, many(p - 1, PAIRS))
                            wait(pe, w3_ready, many(p - 2, PAIRS))

                    if j == 3 and on(p - 2):
                        o_bank_free()
                        wait(pe, step, WEIGHTS * (p - 2) + CHOICES)
                        mm(aux[:, 0:2 * ED], upto[:], taken[:].rearrange("p b e -> p (b e)"), start=True, stop=False)
                        mm(aux[:, 0:2 * ED], ones[:], carry[:, 0:2, :].rearrange("p b e -> p (b e)"),
                           start=False, stop=True).then_inc(count_mm, 1)
                    if j == 5 and on(p + 1):
                        o_bank_free()
                        if at(p, -1):
                            pe.wait_ge(made, 1)
                        wait(pe, xn_ready, 2 * (p + 1) + 2)
                        for b in range(2):
                            last = nc.tensor.transpose(aux[:, b * P:(b + 1) * P], xn[:, b, :], ident[:])
                        last.then_inc(xt_mm, 1)
                    if j == 6 and on(p - 1):
                        o_bank_free()
                        wait(pe, x2n_ready, 2 * p)
                        for b in range(2):
                            last = nc.tensor.transpose(aux[:, b * P:(b + 1) * P], x2n[:, b, :], ident[:])
                        last.then_inc(x2_mm, 1)
                    if j == 7 and (on(p - 1) or on(p - 2)):
                        o_bank_free()
                    if j == 7 and on(p - 2):
                        wait(pe, step, WEIGHTS * (p - 1))
                        for b in range(2):
                            last = nc.tensor.transpose(aux_b[0:W3K, P + b * P:2 * P + b * P], w3[:, b, :], ident_b[:])
                        last.then_inc(w3_mm, 1)
                    if j == 7 and on(p - 1):
                        if at(p, 1):
                            pe.wait_ge(d_gate, 16)
                        wait(pe, x2t_ready, p)
                        for b in range(2):
                            last = mm(aux[:, b * E:(b + 1) * E], x2t[:, b * P:(b + 1) * P], gate[:],
                                      start=True, stop=True)
                        last.then_inc(logit_mm, 1)
                    q, u = shift(p, j, -3)
                    if on(q):
                        g, b = u // 2, u % 2
                        o_bank_free()
                        wait(pe, pt_done, UNITS * q + u + 1)
                        wait(pe, v_ready, 4 * q + 2 * (g // 2) + b + 1)
                        for h in range(4):
                            half = (h % 2) * DH
                            last = mm(o_ps[half:half + DH, (h // 2) * P:(h // 2) * P + P],
                                      v[:, b, (4 * g + h) * DH:(4 * g + h + 1) * DH], prob_t[:, u % 2, h, :],
                                      start=True, stop=True)
                        last.then_inc(av_done, 1)
                    q, u = shift(p, j, -4)
                    if on(q):
                        g, b = u // 2, u % 2
                        if at(q, 0) and u == 0:
                            pe.wait_ge(d_wo, 16)
                        wait(pe, ot_done, UNITS * q + u + 1)
                        if u == 0:
                            wait(pe, x1_done, q)
                        for c in range(2):
                            last = mm(acc_ps[:, b * P:(b + 1) * P], ot[:, u % 2, c, :], wo[:, 2 * g + c, :],
                                      start=(u == 0 and c == 0), stop=(g == GROUPS - 1 and c == 1),
                                      skip_group_check=True)
                        last.then_inc(wo_done, 1)
                    q, vi = {7: (p + 1, 0), 0: (p, 1), 3: (p, 2), 4: (p, 3)}.get(j, (PAIRS, 0))
                    if on(q):
                        b, half = vi % 2, (vi // 2) * 512
                        if at(p, -1):
                            pe.wait_ge(wv_split, 2)
                        wait(pe, ctxv_ready, 2 * q + 2)
                        wait(pe, v_ready, 4 * q + vi)
                        split_mm(v_ps[:], ctxv_hi[:, b * P:(b + 1) * P], ctxv_lo[:, b * P:(b + 1) * P],
                                 wv_hi[:, half:half + 512], wv_lo[:, half:half + 512]).then_inc(v_mm, 1)

                for p in (-1, 0, 1):
                    for j in range(UNITS):
                        slot(p, j)
                with pe.Fori(2, PAIRS - 1) as p:
                    for j in range(UNITS):
                        slot(p, j)
                for p in (PAIRS - 1, PAIRS, PAIRS + 1):
                    for j in range(UNITS):
                        slot(p, j)

                for n in range(BESIDE, FC * FG):
                    chunk(n)
                for n in range(FC * FG - LAG, FC * FG):
                    project(n)


def kernel(x, ctx_1024, L0_xattn_W_q, L0_xattn_W_k, L0_xattn_W_v, L0_xattn_W_o, L0_xattn_b_o, L0_ffn_gate_w,
           L0_ffn_dyn_gate_w, L0_ffn_dyn_up_w, L0_ffn_dyn_down_w, L0_ffn_sh_gate_w, L0_ffn_sh_up_w,
           L0_ffn_sh_down_w):
    import numpy as np
    import concourse.bacc as bacc
    from concourse.bass_utils import run_bass_kernel_spmd

    def lay(a):
        return np.ascontiguousarray(a)

    x, ctx = np.asarray(x), np.asarray(ctx_1024)
    D = x.shape[-1]
    inner = L0_xattn_W_q.shape[1]
    heads = inner // DH

    def by_head(wt):
        return lay(np.asarray(wt).T.reshape(heads, DH, D).transpose(1, 0, 2).reshape(DH, heads * D))

    def rows(dyn, shared):
        return lay(np.concatenate([np.asarray(dyn).reshape(-1, D), np.asarray(shared).reshape(-1, D)]).T)

    def down(dyn, shared):
        units = np.concatenate([np.asarray(a).transpose(0, 2, 1).reshape(-1, D) for a in (dyn, shared)])
        return lay(units.reshape(-1, P, D).transpose(1, 0, 2).reshape(P, -1))

    arrays = {
        "x_in": lay(x),
        "ctx_t": lay(ctx.reshape(-1, D).T),
        "wq_t": by_head(L0_xattn_W_q),
        "wk_t": by_head(L0_xattn_W_k),
        "w_v": lay(L0_xattn_W_v),
        "w_o": lay(L0_xattn_W_o),
        "b_o": lay(np.asarray(L0_xattn_b_o).reshape(1, D)),
        "gate_t": lay(np.asarray(L0_ffn_gate_w).T),
        "wg_t": rows(L0_ffn_dyn_gate_w, L0_ffn_sh_gate_w),
        "wu_t": rows(L0_ffn_dyn_up_w, L0_ffn_sh_up_w),
        "wd_t": down(L0_ffn_dyn_down_w, L0_ffn_sh_down_w),
    }
    nc = bacc.Bacc("TRN2", target_bir_lowering=False, num_devices=1)
    aps = [nc.dram_tensor(k, a.shape, F32, kind="ExternalInput").ap() for k, a in arrays.items()]
    out = nc.dram_tensor("out", x.shape, F32, kind="ExternalOutput").ap()
    xattn_moe(nc, *aps, out)
    r = run_bass_kernel_spmd(nc, [arrays], core_ids=[0])
    return r.results[0]["out"]
```

```python
from contextlib import ExitStack

import concourse.bass as bass
from concourse import mybir

F32 = mybir.dt.float32
F32R = mybir.dt.float32r
BF16 = mybir.dt.bfloat16
ALU = mybir.AluOpType
ACT = mybir.ActivationFunctionType
X = mybir.AxisListType.X

P = 128
DH = 64
TOP_K = 4
TOP_P = 0.75
JITTER = 0.2
EPS = 1e-5
HIDE = 1e30



def xattn_moe(nc, x, ctx_t, wq_t, wk_t, w_v, w_o, b_o, gate_t, wg_t, wu_t, wd_t, out_t):
    B = x.shape[0]
    T = B * P
    H = wq_t.shape[1] // P
    PAIRS = B // 2
    GROUPS = H // 4
    UNITS = 2 * GROUPS
    E = gate_t.shape[1]
    ED = E - 1
    FC = wd_t.shape[1] // P
    CAP = max(-(-T * 5 // (4 * ED)), 4)
    TB = 4
    FG = B // TB
    HALF = H // 2 * P
    WPIECE = FC * P // 3
    W3 = 32
    W3K = 3 * W3
    FIRST_CHUNK = 1
    BESIDE = 2 * UNITS - FIRST_CHUNK
    LAG = 4
    RING = LAG + 2
    SHARED = ED // 2
    PICKS = SHARED + 1
    assert GROUPS == 4 and FC == 6 and B % 4 == 0

    def on(q):
        return 0 <= q < PAIRS if isinstance(q, int) else True

    def at(p, first):
        return isinstance(p, int) and p == first

    def shift(p, j, d):
        t = j + d
        return p + t // UNITS, t % UNITS

    def wait(eng, sem, value):
        if not isinstance(value, int) or value > 0:
            eng.wait_ge(sem, value)

    def many(value, most):
        return max(0, min(most, value)) if isinstance(value, int) else value

    def chunk_beside(p, j):
        n = UNITS * (p - PAIRS) + j - FIRST_CHUNK if isinstance(p, int) else -1
        return n if n >= 0 else None

    def last_of_pick(m):
        return FC * (m // PICKS) + (FC - 1 if m % PICKS == SHARED else m % PICKS)

    def v_chunk(p, j):
        if j == 7 and not at(p, -1):
            return p + 1, 0
        first_pair = {0: 0, 1: 1} if at(p, 0) else {0: 1}
        quarter = {**first_pair, 3: 2, 4: 3}.get(j)
        return (PAIRS, 0) if quarter is None else (p, quarter)

    def cols(q, n):
        return bass.ds(q * n, n)

    with ExitStack() as ctx:
        def sb(name, shape, dt=F32):
            return ctx.enter_context(nc.sbuf_tensor(name, shape, dt))

        def psum(name, shape):
            return ctx.enter_context(nc.psum_tensor(name, shape, F32))

        def sem(name):
            return ctx.enter_context(nc.semaphore(name))

        x_all = sb("x_all", [P, B, P])
        ctx_all = sb("ctx_all", [P, T])
        wq = sb("wq", [DH, H * P])
        wk = sb("wk", [DH, H * P])
        wv = sb("wv", [P, H * DH])
        wo = sb("wo", [P, H // 2, P])
        bo = sb("bo", [P, P])
        gate = sb("gate", [P, E])
        wg = sb("wg", [P, FC * P])
        wu = sb("wu", [P, FC * P])
        wd = sb("wd", [P, FC * P])
        ctx_hi = sb("ctx_hi", [P, T], F32R)
        ctx_lo = sb("ctx_lo", [P, T], F32R)
        ctxv_hi = sb("ctxv_hi", [P, 2 * P], F32R)
        ctxv_lo = sb("ctxv_lo", [P, 2 * P], F32R)
        a_parts = sb("a_parts", [P, 2, H, P], F32R)
        a_hi, a_lo = a_parts[:, 0], a_parts[:, 1]
        wv_hi = sb("wv_hi", [P, H * DH], F32R)
        wv_lo = sb("wv_lo", [P, H * DH], F32R)
        wg_hi = sb("wg_hi", [P, FC * P], F32R)
        wg_lo = sb("wg_lo", [P, FC * P], F32R)
        wu_hi = sb("wu_hi", [P, FC * P], F32R)
        wu_lo = sb("wu_lo", [P, FC * P], F32R)
        wd_hi = sb("wd_hi", [P, FC * P], F32R)
        wd_lo = sb("wd_lo", [P, FC * P], F32R)
        z_parts = sb("z_parts", [P, 2, 2, 4, 2, P], F32R)
        z_hi, z_lo = z_parts[:, 0], z_parts[:, 1]
        xt_hi = sb("xt_hi", [P, 2, P], F32R)
        xt_lo = sb("xt_lo", [P, 2, P], F32R)
        x2_hi = sb("x2_hi", [P, T], F32R)
        x2_lo = sb("x2_lo", [P, T], F32R)
        stat1 = sb("stat1", [P, 2, 6])
        mv1 = sb("mv1", [P, 2, 2])
        var1 = sb("var1", [P, 2])
        rstd1 = sb("rstd1", [P, 2])
        xn = sb("xn", [P, 2, P])
        xt = sb("xt", [P, 2 * P])
        neg_max = sb("neg_max", [P, 2, 4])
        row_sum = sb("row_sum", [P, 2, 4])
        row_inv = sb("row_inv", [P, 2, 4])
        prob = sb("prob", [P, 2, 4, P])
        prob_n = sb("prob_n", [P, 2, 4, P])
        prob_t = sb("prob_t", [P, 2, 4, P])
        v = sb("v", [P, 2, H * DH])
        ot = sb("ot", [P, 2, 2, P])
        xb = sb("xb", [P, 2, P])
        x1 = sb("x1", [P, 2, P])
        x1t_all = sb("x1t_all", [P, T])
        stat2 = sb("stat2", [P, 2, 6])
        mv2 = sb("mv2", [P, 2, 2])
        var2 = sb("var2", [P, 2])
        rstd2 = sb("rstd2", [P, 2])
        x2n = sb("x2n", [P, 2, P])
        x2t = sb("x2t", [P, 2 * P])
        logit = sb("logit", [P, 2, E])
        size = sb("size", [P, 2, ED])
        gap = sb("gap", [P, 2, ED, ED])
        big = sb("big", [P, 2, ED, ED])
        keep = sb("keep", [P, 2, ED, ED])
        tie = sb("tie", [P, 2, ED, ED])
        ahead = sb("ahead", [P, 2, ED, ED])
        gap0 = sb("gap0", [P, 2, ED, ED])
        near = sb("near", [P, 2, ED, ED])
        e_gap = sb("e_gap", [P, 2, ED, ED])
        e_near = sb("e_near", [P, 2, ED, ED])
        e_ahead = sb("e_ahead", [P, 2, ED, ED])
        denom = sb("denom", [P, 2, ED])
        rank = sb("rank", [P, 2, ED])
        top = sb("top", [P, 2])
        below = sb("below", [P, 2, ED])
        e_dyn = sb("e_dyn", [P, 2, ED])
        mass = sb("mass", [P, 2, ED])
        total = sb("total", [P, 2])
        small = sb("small", [P, 2, ED])
        valid = sb("valid", [P, 2, ED])
        mult = sb("mult", [P, 2, ED])
        mult_v = sb("mult_v", [P, 2, ED])
        mult_sum = sb("mult_sum", [P, 2])
        mult_inv = sb("mult_inv", [P, 2])
        rw = sb("rw", [P, 2, ED])
        taken = sb("taken", [P, 2, ED], BF16)
        carry = sb("carry", [P, 3, ED], BF16)
        count = sb("count", [P, 2, ED])
        fits = sb("fits", [P, 2, ED])
        shown = sb("shown", [P, 2, ED])
        hidden = sb("hidden", [P, 2, ED])
        masked = sb("masked", [P, 2, E])
        top2 = sb("top2", [P, 2])
        below2 = sb("below2", [P, 2, E])
        e_all = sb("e_all", [P, 2, E])
        total2 = sb("total2", [P, 2])
        total_dyn = sb("total_dyn", [P, 2])
        inv2 = sb("inv2", [P, 2])
        share_dyn = sb("share_dyn", [P, 2])
        gd = sb("gd", [P, 2, ED])
        w = sb("w", [P, 2, E])
        w_rest = sb("w_rest", [P, 2, E])
        w3 = sb("w3", [P, 2, W3K], BF16)
        w3_all = sb("w3_all", [W3K, T], BF16)
        act = sb("act", [P, 2, TB * P])
        hid = sb("hid", [P, 2, TB * P])
        hid_hi = a_parts[:].rearrange("p s h d -> p (s h d)").rearrange("p (k t) -> p k t", t=TB * P)
        hid_lo = z_parts[:].rearrange("p s r h b m -> p (s r h b m)").rearrange("p (k t) -> p k t", t=TB * P)
        gu = ctx_all[:, 0:2 * TB * P].rearrange("p (k t) -> p k t", k=2)
        y = ctx_all[:, 2 * TB * P:4 * TB * P].rearrange("p (k t) -> p k t", k=2)
        ident = sb("ident", [P, P])
        ident_b = sb("ident_b", [P, P], BF16)
        upto = sb("upto", [P, P], BF16)
        ones = sb("ones", [P, P], BF16)
        first = sb("first", [P, 2, ED, ED])
        pick = sb("pick", [W3K, PICKS, P], BF16)
        warm = sb("warm", [P, 2])
        power = sb("power", [P, 2])
        eps = sb("eps", [P, 2])

        z_ps = psum("z_ps", [P, 2, 512])
        s_ps = psum("s_ps", [P, 2, 512])
        t_ps = psum("t_ps", [P, 512])
        o_ps = psum("o_ps", [P, 512])
        acc_ps = psum("acc_ps", [P, 512])
        v_ps = psum("v_ps", [P, 512])
        aux = o_ps[:, 256:512]
        w_bank = [v_ps[:], t_ps[:]]
        a_bank = [z_ps[:, 0, :], z_ps[:, 1, :], t_ps[:], acc_ps[:]]
        aux_b = aux.bitcast(BF16)

        d_wk0, d_wq0, d_wk, d_wq, d_ctx0, d_ctx, d_x0, d_x, d_wv, d_wo, d_bo, d_gate, d_wg, d_wu, d_wd = (
            sem("d_" + n) for n in "wk0 wq0 wk wq ctx0 ctx x0 x wv wo bo gate wg wu wd".split())
        zeroed, made = sem("zeroed"), sem("made")
        ctx_split = sem("ctx_split")
        a_mm, a_hi_done, a_lo_done = sem("a_mm"), sem("a_hi_done"), sem("a_lo_done")
        wv_split = sem("wv_split")
        w_split = sem("w_split")
        last_low_done = sem("last_low_done")
        ctxv_ready = sem("ctxv_ready")
        ln1, ln1_rstd, xn_ready, xt_mm, xt_ready, xt_split = (
            sem(n) for n in "ln1 ln1_rstd xn_ready xt_mm xt_ready xt_split".split())
        z_mm, z_hi_done, z_lo_done = sem("z_mm"), sem("z_hi_done"), sem("z_lo_done")
        s_done, max_done, exp_done, inv_done, norm_done = (
            sem(n) for n in "s_done max_done exp_done inv_done norm_done".split())
        t_done, pt_done, av_done, ot_done, wo_done = (
            sem(n) for n in "t_done pt_done av_done ot_done wo_done".split())
        v_mm, v_ready = sem("v_mm"), sem("v_ready")
        xb_ready, x1_done, x1t_mm, x1_kept = sem("xb_ready"), sem("x1_done"), sem("x1t_mm"), sem("x1_kept")
        ln2, ln2_rstd, x2n_ready, x2_mm, x2t_ready, x2_split = (
            sem(n) for n in "ln2 ln2_rstd x2n_ready x2_mm x2t_ready x2_split".split())
        logit_mm, logit_ready = sem("logit_mm"), sem("logit_ready")
        step, router_exp = sem("step"), sem("router_exp")
        count_mm, count_ready = sem("count_mm"), sem("count_ready")
        w3_mm, w3_ready = sem("w3_mm"), sem("w3_ready")
        g_mm, u_mm, wb_mm, silu_done, gu_done, hid_done, hid_hi_done, hid_lo_done, down_done, y_done = (
            sem(n) for n in "g_mm u_mm wb_mm silu_done gu_done hid_done hid_hi_done hid_lo_done down_done y_done"
            .split())
        stored = [sem(f"stored{k}") for k in range(2)]

        GAPS, CHOICES, FITTING, WEIGHTS = 5, 23, 34, 46

        with nc.Block() as block:
            @block.sync
            def _(sp):
                x_v = x.rearrange("b t d -> t b d")
                sp.dma_start(wk[:, 0:HALF], wk_t[:, 0:HALF]).then_inc(d_wk0, 16)
                sp.dma_start(ctx_all[:, 0:2 * P], ctx_t[:, 0:2 * P]).then_inc(d_ctx0, 16)
                sp.dma_start(wk[:, HALF:], wk_t[:, HALF:]).then_inc(d_wk, 16)
                sp.dma_start(wv[:], w_v).then_inc(d_wv, 16)
                sp.dma_start(ctx_all[:, 2 * P:T], ctx_t[:, 2 * P:T]).then_inc(d_ctx, 16)
                sp.dma_start(x_all[:, 2:B, :], x_v[:, 2:B, :]).then_inc(d_x, 16)
                sp.dma_start(bo[:], b_o.to_broadcast([P, P])).then_inc(d_bo, 16)
                sp.dma_start(gate[:], gate_t).then_inc(d_gate, 16)
                sp.dma_start(wo[:], w_o.rearrange("(c p) d -> p c d", p=P)).then_inc(d_wo, 16)
                sp.dma_start(wg[:], wg_t).then_inc(d_wg, 16)
                sp.dma_start(wu[:], wu_t).then_inc(d_wu, 16)
                sp.dma_start(wd[:], wd_t).then_inc(d_wd, 16)
                for g in range(FG):
                    sp.wait_ge(y_done, g + 1)
                    sp.dma_start(out_t[:, cols(g, TB * P)], y[:, g % 2, :]).then_inc(stored[g % 2], 16)
                for k in range(2):
                    sp.wait_ge(stored[k], 16 * (FG // 2))

            @block.gpsimd
            def _(pool):
                nc.gpsimd.memset(ident[:], 0.0).then_inc(zeroed, 1)
                nc.gpsimd.memset(power[:], -0.5).then_inc(zeroed, 1)
                nc.gpsimd.memset(eps[:], EPS).then_inc(zeroed, 1)
                pool.wait_ge(zeroed, 3)
                nc.gpsimd.affine_select(out=ident[:], in_=ident[:], compare_op=ALU.not_equal, fill=1.0, base=0,
                                        pattern=[[-1, P]], channel_multiplier=1).then_inc(made, 1)
                nc.gpsimd.memset(ident_b[:], 0.0).then_inc(zeroed, 1)
                nc.gpsimd.memset(upto[:], 0.0).then_inc(zeroed, 1)
                nc.gpsimd.memset(first[:], 0.0).then_inc(zeroed, 1)
                nc.gpsimd.memset(pick[:], 0.0).then_inc(zeroed, 1)
                nc.gpsimd.memset(w3[:], 0.0).then_inc(zeroed, 1)
                nc.gpsimd.memset(carry[:], 0.0).then_inc(zeroed, 1)
                nc.gpsimd.memset(ones[:], 1.0).then_inc(zeroed, 1)
                pool.wait_ge(zeroed, 10)
                nc.gpsimd.affine_select(out=ident_b[:], in_=ident_b[:], compare_op=ALU.not_equal, fill=1.0,
                                        base=0, pattern=[[-1, P]], channel_multiplier=1).then_inc(made, 1)
                nc.gpsimd.affine_select(out=upto[:], in_=upto[:], compare_op=ALU.is_gt, fill=1.0, base=0,
                                        pattern=[[-1, P]], channel_multiplier=1).then_inc(made, 1)
                nc.gpsimd.affine_select(out=first[:], in_=first[:], compare_op=ALU.is_ge, fill=1.0, base=0,
                                        pattern=[[0, 2], [-1, ED], [1, ED]], channel_multiplier=0).then_inc(made, 1)

                for part in range(3):
                    pool.wait_ge(made, 4 + 2 * part)
                    rows = pick[W3 * part:W3 * part + W3]
                    dyn = rows[:, 0:ED // 2, :].rearrange("r c (h i) -> r c h i", h=2)
                    nc.gpsimd.affine_select(out=dyn, in_=dyn, compare_op=ALU.not_equal, fill=1.0, base=0,
                                            pattern=[[-2, ED // 2], [-1, 2], [0, DH]],
                                            channel_multiplier=1).then_inc(made, 1)
                    shared = rows[:, ED // 2, :]
                    nc.gpsimd.affine_select(out=shared, in_=shared, compare_op=ALU.not_equal, fill=1.0,
                                            base=-ED, pattern=[[0, P]], channel_multiplier=1).then_inc(made, 1)
                pool.wait_ge(made, 10)

                def split_weights(src, hi, lo, landed, n, piece):
                    unit = cols(piece, WPIECE)
                    pool.wait_ge(landed, 16)
                    nc.gpsimd.tensor_copy(hi[:, unit], src[:, unit]).then_inc(w_split, 1)
                    pool.wait_ge(w_split, n + 1)
                    nc.gpsimd.tensor_tensor(lo[:, unit], src[:, unit], hi[:, unit].bitcast(F32),
                                            ALU.subtract).then_inc(w_split, 1)

                def chunk(n):
                    pool.wait_ge(hid_hi_done, n + 1)
                    nc.gpsimd.tensor_tensor(hid_lo[:, n % RING, :], hid[:, n % 2, :],
                                            hid_hi[:, n % RING, :].bitcast(F32), ALU.subtract).then_inc(hid_lo_done, 1)

                def slot(p, j):
                    if j == 2 and on(p + 1):
                        q = p + 1
                        wait(pool, ln1, 4 * q + 4)
                        nc.gpsimd.tensor_tensor(var1[:], mv1[:, :, 1], eps[:], ALU.add).then_inc(ln1_rstd, 1)
                        wait(pool, ln1_rstd, 2 * q + 1)
                        nc.gpsimd.tensor_tensor(rstd1[:], var1[:], power[:], ALU.pow).then_inc(ln1_rstd, 1)
                    if j == 5 and on(p - 1):
                        q = p - 1
                        wait(pool, ln2, 4 * q + 4)
                        nc.gpsimd.tensor_tensor(var2[:], mv2[:, :, 1], eps[:], ALU.add).then_inc(ln2_rstd, 1)
                        wait(pool, ln2_rstd, 2 * q + 1)
                        nc.gpsimd.tensor_tensor(rstd2[:], var2[:], power[:], ALU.pow).then_inc(ln2_rstd, 1)
                    q, u = shift(p, j, -1)
                    if on(q):
                        n = UNITS * q + u
                        wait(pool, inv_done, n + 1)
                        wait(pool, t_done, n - 1)
                        nc.gpsimd.tensor_tensor(prob_n[:, u % 2], prob[:, u % 2],
                                                row_inv[:, u % 2, :].unsqueeze(2).to_broadcast([P, 4, P]),
                                                ALU.mult).then_inc(norm_done, 1)
                    if j == 6 and on(p):
                        if at(p, 0):
                            pool.wait_ge(d_bo, 16)
                            pool.wait_ge(d_x0, 16)
                            pool.wait_ge(d_x, 16)
                        wait(pool, x1_done, p)
                        nc.gpsimd.tensor_tensor(xb[:], x_all[:, cols(p, 2), :],
                                                bo[:].unsqueeze(1).to_broadcast([P, 2, P]),
                                                ALU.add).then_inc(xb_ready, 1)
                    if j == 5 and on(p + 1):
                        q = p + 1
                        if at(q, 0):
                            pool.wait_ge(ctx_split, 2)
                        if at(q, 1):
                            pool.wait_ge(ctx_split, 4)
                        if at(q, 2):
                            pool.wait_ge(ctx_split, 10)
                        wait(pool, v_mm, 4 * q)
                        nc.gpsimd.tensor_copy(ctxv_hi[:], ctx_hi[:, cols(q, 2 * P)]).then_inc(ctxv_ready, 1)
                        nc.gpsimd.tensor_copy(ctxv_lo[:], ctx_lo[:, cols(q, 2 * P)]).then_inc(ctxv_ready, 1)
                    if j == 7 and on(p - 1):
                        q = p - 1
                        wait(pool, x2t_ready, q + 1)
                        nc.gpsimd.tensor_copy(x2_hi[:, cols(q, 2 * P)], x2t[:]).then_inc(x2_split, 1)
                        wait(pool, x2_split, 2 * q + 1)
                        nc.gpsimd.tensor_tensor(x2_lo[:, cols(q, 2 * P)], x2t[:],
                                                x2_hi[:, cols(q, 2 * P)].bitcast(F32),
                                                ALU.subtract).then_inc(x2_split, 1)
                    if at(p, -1) and j == 5:
                        pool.wait_ge(d_wv, 16)
                        pool.wait_ge(wv_split, 1)
                        nc.gpsimd.tensor_tensor(wv_lo[:], wv[:], wv_hi[:].bitcast(F32),
                                                ALU.subtract).then_inc(wv_split, 1)
                    if at(p, 0) and j in (1, 4, 7):
                        piece = (1, 4, 7).index(j)
                        split_weights(wg, wg_hi, wg_lo, d_wg, 2 * piece, piece)
                    if at(p, 1) and j in (0, 1, 3):
                        piece = (0, 1, 3).index(j)
                        split_weights(wu, wu_hi, wu_lo, d_wu, 6 + 2 * piece, piece)
                    if at(p, PAIRS) and j < 3:
                        split_weights(wd, wd_hi, wd_lo, d_wd, 12 + 2 * j, j)
                    if chunk_beside(p, j - 2) is not None:
                        chunk(chunk_beside(p, j - 2))

                for p in (-1, 0, 1):
                    for j in range(UNITS):
                        slot(p, j)
                with pool.Fori(2, PAIRS - 1) as p:
                    for j in range(UNITS):
                        slot(p, j)
                for p in (PAIRS - 1, PAIRS, PAIRS + 1):
                    for j in range(UNITS):
                        slot(p, j)

                for n in range(BESIDE - 2, FC * FG - 1):
                    chunk(n)

            @block.scalar
            def _(sc):
                sc.dma_start(wq[:, 0:HALF], wq_t[:, 0:HALF]).then_inc(d_wq0, 16)
                sc.dma_start(x_all[:, 0:2, :], x.rearrange("b t d -> t b d")[:, 0:2, :]).then_inc(d_x0, 16)
                sc.dma_start(wq[:, HALF:], wq_t[:, HALF:]).then_inc(d_wq, 16)
                def a_high(g):
                    sc.wait_ge(a_mm, g + 1)
                    nc.scalar.activation(a_hi[:, 4 * g:4 * g + 4, :].rearrange("p h d -> p (h d)"), a_bank[g],
                                         ACT.Copy, scale=DH ** -0.5).then_inc(a_hi_done, 1)

                sc.wait_ge(zeroed, 3)
                nc.scalar.activation(warm[:], eps[:], ACT.Exp)
                a_high(0)
                a_high(1)
                sc.wait_ge(d_wv, 16)
                nc.scalar.activation(wv_hi[:], wv[:], ACT.Copy).then_inc(wv_split, 1)

                def chunk(n):
                    c = n % FC
                    sc.wait_ge(g_mm, n + 1)
                    wait(sc, gu_done, n - 1)
                    nc.scalar.activation(act[:, c % 2, :], z_ps[:, c % 2, :], ACT.Silu).then_inc(silu_done, 1)
                    if n > 0:
                        hid_high(n - 1)

                def hid_high(n):
                    wait(sc, hid_done, n + 1)
                    wait(sc, down_done, n - RING + 1)
                    nc.scalar.activation(hid_hi[:, n % RING, :], hid[:, n % 2, :], ACT.Copy).then_inc(hid_hi_done, 1)

                def slot(p, j):
                    if chunk_beside(p, j - 1) is not None:
                        chunk(chunk_beside(p, j - 1))
                    if j == 1 and on(p - 2):
                        wait(sc, step, WEIGHTS * (p - 2) + GAPS)
                        nc.scalar.activation(e_gap[:], gap0[:], ACT.Exp, scale=-1.0).then_inc(router_exp, 1)
                        nc.scalar.activation(e_dyn[:], below[:], ACT.Exp).then_inc(router_exp, 1)
                    q, z = shift(p, j, 3)
                    if on(q):
                        wait(sc, z_mm, UNITS * q + z + 1)
                        wait(sc, s_done, UNITS * q + 2 * (z // 2) - 2)
                        nc.scalar.activation(
                            z_hi[:, (z // 2) % 2, 2 * (z % 2):2 * (z % 2) + 2].rearrange("p h b m -> p (h b m)"),
                            z_ps[:, z % 2, :], ACT.Copy).then_inc(z_hi_done, 1)
                    if on(p):
                        n = UNITS * p + j
                        wait(sc, max_done, n + 1)
                        wait(sc, norm_done, n - 1)
                        for h in range(4):
                            last = nc.scalar.activation(
                                prob[:, j % 2, h, :], s_ps[:, j % 2, h * P:(h + 1) * P], ACT.Exp,
                                bias=neg_max[:, j % 2, h:h + 1], accum_out=row_sum[:, j % 2, h:h + 1])
                        last.then_inc(exp_done, 1)
                    if j == 5 and on(p - 2):
                        wait(sc, step, WEIGHTS * (p - 2) + FITTING)
                        nc.scalar.activation(e_all[:], below2[:], ACT.Exp).then_inc(router_exp, 1)
                    q, u = shift(p, j, -2)
                    if on(q) and u % 2:
                        n = UNITS * q + u
                        wait(sc, t_done, n + 1)
                        wait(sc, av_done, n - 1)
                        nc.scalar.activation(prob_t[:, 1].rearrange("p h t -> p (h t)"), t_ps[:],
                                             ACT.Copy).then_inc(pt_done, 1)
                    q, u = shift(p, j, -3)
                    if on(q):
                        wait(sc, av_done, UNITS * q + u + 1)
                    if j == 1 and on(p - 2):
                        wait(sc, x1t_mm, p - 1)
                        nc.scalar.activation(x1t_all[:, cols(p - 2, 2 * P)], aux, ACT.Copy).then_inc(x1_kept, 1)
                    if j == 3 and on(p - 2):
                        wait(sc, count_mm, p - 1)
                        nc.scalar.activation(count[:].rearrange("p b e -> p (b e)"), aux[:, 0:2 * ED],
                                             ACT.Copy).then_inc(count_ready, 1)
                    if j == 5 and on(p + 1):
                        wait(sc, xt_mm, p + 2)
                        wait(sc, xt_split, 4 * (p + 1))
                        nc.scalar.activation(xt[:], aux, ACT.Copy).then_inc(xt_ready, 1)
                    if j == 6 and on(p - 1):
                        wait(sc, x2_mm, p)
                        wait(sc, x2_split, 2 * (p - 1))
                        wait(sc, logit_mm, p - 1)
                        nc.scalar.activation(x2t[:], aux, ACT.Copy).then_inc(x2t_ready, 1)
                    if j == 7 and on(p - 1):
                        wait(sc, logit_mm, p)
                        wait(sc, step, WEIGHTS * (p - 1))
                        nc.scalar.activation(logit[:].rearrange("p b e -> p (b e)"), aux[:, 0:2 * E],
                                             ACT.Copy).then_inc(logit_ready, 1)
                    if j == 7 and on(p - 2):
                        wait(sc, w3_mm, p - 1)
                        nc.scalar.activation(w3_all[:, cols(p - 2, 2 * P)], aux_b[0:W3K, P:P + 2 * P],
                                             ACT.Copy).then_inc(w3_ready, 1)
                    if on(q):
                        n = UNITS * q + u
                        wait(sc, wo_done, n - 1)
                        nc.scalar.activation(ot[:, u % 2].rearrange("p c t -> p (c t)"), o_ps[:, 0:256],
                                             ACT.Copy).then_inc(ot_done, 1)
                    q, vi = v_chunk(p, j)
                    if on(q):
                        wait(sc, v_mm, 4 * q + vi + 1)
                        wait(sc, av_done, UNITS * (q - 1) + (2, 3, 6, 7)[vi] + 1)
                        nc.scalar.activation(v[:, vi % 2, (vi // 2) * 512:(vi // 2) * 512 + 512], v_ps[:],
                                             ACT.Copy).then_inc(v_ready, 1)
                    if at(p, -1) and j == 7:
                        a_high(2)
                    if at(p, 0) and j == 0:
                        a_high(3)

                for p in (-1, 0, 1):
                    for j in range(UNITS):
                        slot(p, j)
                with sc.Fori(2, PAIRS - 1) as p:
                    for j in range(UNITS):
                        slot(p, j)
                for p in (PAIRS - 1, PAIRS, PAIRS + 1):
                    for j in range(UNITS):
                        slot(p, j)

                for n in range(BESIDE - 1, FC * FG):
                    chunk(n)
                hid_high(FC * FG - 1)

            @block.vector
            def _(ve):
                def a_low(g):
                    ve.wait_ge(a_hi_done, g + 1)
                    nc.vector.scalar_tensor_tensor(
                        a_lo[:, 4 * g:4 * g + 4, :].rearrange("p h d -> p (h d)"), a_bank[g], DH ** -0.5,
                        a_hi[:, 4 * g:4 * g + 4, :].rearrange("p h d -> p (h d)").bitcast(F32),
                        ALU.mult, ALU.subtract).then_inc(a_lo_done, 1)

                def split_ctx(start, end, n):
                    nc.vector.tensor_copy(ctx_hi[:, start:end], ctx_all[:, start:end]).then_inc(ctx_split, 1)
                    ve.wait_ge(ctx_split, n + 1)
                    nc.vector.tensor_tensor(ctx_lo[:, start:end], ctx_all[:, start:end],
                                            ctx_hi[:, start:end].bitcast(F32), ALU.subtract).then_inc(ctx_split, 1)

                ve.wait_ge(d_ctx0, 16)
                split_ctx(0, 2 * P, 0)

                def flat(a):
                    return a[:].rearrange("p b j i -> p (b j i)")

                def wide(a, n=ED):
                    return a[:].unsqueeze(2).to_broadcast([P, 2, n])

                def of_j(a):
                    return a.unsqueeze(3).to_broadcast([P, 2, ED, ED])

                def of_i(a):
                    return a.unsqueeze(2).to_broadcast([P, 2, ED, ED])

                tensor, two, scale, red = (nc.vector.tensor_tensor, nc.vector.scalar_tensor_tensor,
                                           nc.vector.tensor_scalar, nc.vector.tensor_reduce)
                s = logit[:, :, 0:ED]

                def router(q, j, place):
                    at_place = (j, place)
                    if at_place == (0, 0):
                        wait(ve, logit_ready, q + 1)
                        tensor(gap[:], of_j(s), of_i(s), ALU.subtract).then_inc(step, 1)
                        two(size[:], s, -1.0, s, ALU.mult, ALU.max).then_inc(step, 1)
                        red(top[:], s, X, ALU.max).then_inc(step, 1)
                    if at_place == (0, 1):
                        wait(ve, step, WEIGHTS * q + 3)
                        scale(flat(gap0), flat(gap), 0.0, None, ALU.max).then_inc(step, 1)
                        tensor(below[:], s, wide(top), ALU.subtract).then_inc(step, 1)
                    if at_place == (0, 2):
                        wait(ve, step, WEIGHTS * q + GAPS)
                        tensor(big[:], of_j(size[:]), of_i(size[:]), ALU.max).then_inc(step, 1)
                        two(flat(tie), flat(gap), 0.0, flat(first), ALU.is_equal, ALU.mult).then_inc(step, 1)
                    if at_place == (0, 3):
                        wait(ve, step, WEIGHTS * q + 7)
                        two(flat(ahead), flat(gap), 0.0, flat(tie), ALU.is_lt, ALU.add).then_inc(step, 1)
                        two(flat(keep), flat(big), JITTER, flat(gap), ALU.mult, ALU.is_ge).then_inc(step, 1)
                    if at_place == (1, 0):
                        wait(ve, step, WEIGHTS * q + 9)
                        two(flat(near), flat(ahead), 0.5, flat(keep), ALU.is_lt, ALU.mult).then_inc(step, 1)
                    if at_place == (1, 3):
                        wait(ve, step, WEIGHTS * q + 10)
                        wait(ve, router_exp, 3 * q + 2)
                        tensor(flat(e_near), flat(e_gap), flat(near), ALU.mult).then_inc(step, 1)
                        red(rank[:], ahead[:], X, ALU.add).then_inc(step, 1)
                        red(total[:], e_dyn[:], X, ALU.add).then_inc(step, 1)
                        tensor(e_ahead[:], ahead[:], of_i(e_dyn[:]), ALU.mult).then_inc(step, 1)
                    if at_place == (2, 0):
                        wait(ve, step, WEIGHTS * q + 14)
                        red(denom[:], e_near[:], X, ALU.add).then_inc(step, 1)
                        red(mass[:], e_ahead[:], X, ALU.add).then_inc(step, 1)
                    if at_place == (2, 1):
                        wait(ve, step, WEIGHTS * q + 16)
                        nc.vector.reciprocal(mult[:], denom[:]).then_inc(step, 1)
                        two(small[:], wide(total), TOP_P, mass[:], ALU.mult, ALU.is_gt).then_inc(step, 1)
                    if at_place == (2, 2):
                        wait(ve, step, WEIGHTS * q + 18)
                        two(valid[:], rank[:], float(TOP_K), small[:], ALU.is_lt, ALU.mult).then_inc(step, 1)
                    if at_place == (2, 3):
                        wait(ve, step, WEIGHTS * q + 19)
                        nc.vector.tensor_copy(taken[:], valid[:]).then_inc(step, 1)
                        tensor(mult_v[:], mult[:], valid[:], ALU.mult).then_inc(step, 1)
                        nc.vector.tensor_copy(carry[:, 0, :], carry[:, 2, :]).then_inc(step, 1)
                    if at_place == (3, 0):
                        wait(ve, step, WEIGHTS * q + 22)
                        tensor(carry[:, 1, :], carry[:, 0, :], taken[:, 0, :], ALU.add).then_inc(step, 1)
                    if at_place == (3, 1):
                        wait(ve, step, WEIGHTS * q + CHOICES)
                        tensor(carry[:, 2, :], carry[:, 1, :], taken[:, 1, :], ALU.add).then_inc(step, 1)
                        red(mult_sum[:], mult_v[:], X, ALU.add).then_inc(step, 1)
                    if at_place == (4, 1):
                        wait(ve, step, WEIGHTS * q + 25)
                        wait(ve, count_ready, q + 1)
                        two(fits[:], count[:], float(CAP), valid[:], ALU.is_le, ALU.mult).then_inc(step, 1)
                    if at_place == (4, 2):
                        wait(ve, step, WEIGHTS * q + 26)
                        tensor(shown[:], s, fits[:], ALU.mult).then_inc(step, 1)
                        scale(hidden[:], fits[:], 1.0, HIDE, ALU.subtract, ALU.mult).then_inc(step, 1)
                        nc.vector.tensor_copy(masked[:, :, ED:E], logit[:, :, ED:E]).then_inc(step, 1)
                        nc.vector.reciprocal(mult_inv[:], mult_sum[:]).then_inc(step, 1)
                    if at_place == (4, 3):
                        wait(ve, step, WEIGHTS * q + 30)
                        tensor(masked[:, :, 0:ED], shown[:], hidden[:], ALU.add).then_inc(step, 1)
                        tensor(rw[:], mult_v[:], wide(mult_inv), ALU.mult).then_inc(step, 1)
                    if at_place == (5, 0):
                        wait(ve, step, WEIGHTS * q + 32)
                        red(top2[:], masked[:], X, ALU.max).then_inc(step, 1)
                    if at_place == (5, 1):
                        wait(ve, step, WEIGHTS * q + 33)
                        tensor(below2[:], masked[:], wide(top2, E), ALU.subtract).then_inc(step, 1)
                    if at_place == (5, 3):
                        wait(ve, step, WEIGHTS * q + FITTING)
                        wait(ve, router_exp, 3 * q + 3)
                        red(total2[:], e_all[:], X, ALU.add).then_inc(step, 1)
                        red(total_dyn[:], e_all[:, :, 0:ED], X, ALU.add).then_inc(step, 1)
                    if at_place == (6, 0):
                        wait(ve, step, WEIGHTS * q + 36)
                        nc.vector.reciprocal(inv2[:], total2[:]).then_inc(step, 1)
                    if at_place == (6, 1):
                        wait(ve, step, WEIGHTS * q + 37)
                        if isinstance(q, int):
                            wait(ve, w3_mm, q)
                        tensor(share_dyn[:], total_dyn[:], inv2[:], ALU.mult).then_inc(step, 1)
                        tensor(w[:, :, ED:E], e_all[:, :, ED:E], wide(inv2, 1), ALU.mult).then_inc(step, 1)
                        tensor(w3[:, :, ED:E], e_all[:, :, ED:E], wide(inv2, 1), ALU.mult).then_inc(step, 1)
                    if at_place == (6, 2):
                        wait(ve, step, WEIGHTS * q + 40)
                        tensor(gd[:], rw[:], wide(share_dyn), ALU.mult).then_inc(step, 1)
                        wait(ve, step, WEIGHTS * q + 41)
                        tensor(w[:, :, 0:ED], gd[:], fits[:], ALU.mult).then_inc(step, 1)
                        tensor(w3[:, :, 0:ED], gd[:], fits[:], ALU.mult).then_inc(step, 1)
                    if at_place == (6, 3):
                        wait(ve, step, WEIGHTS * q + 43)
                        tensor(w_rest[:], w[:], w3[:, :, 0:E], ALU.subtract).then_inc(step, 1)
                    if at_place == (7, 0):
                        wait(ve, step, WEIGHTS * q + 44)
                        nc.vector.tensor_copy(w3[:, :, W3:W3 + E], w_rest[:]).then_inc(step, 1)
                        wait(ve, step, WEIGHTS * q + 45)
                        tensor(w3[:, :, 2 * W3:2 * W3 + E], w_rest[:], w3[:, :, W3:W3 + E], ALU.subtract).then_inc(step, 1)

                def residual(g):
                    wait(ve, down_done, FC * g + FC)
                    wait(ve, stored[g % 2], 16 * (g // 2))
                    if g == FG - 1:
                        ve.wait_ge(x1_kept, PAIRS)
                    nc.vector.tensor_tensor(y[:, g % 2, :], acc_ps[:], x1t_all[:, cols(g, TB * P)],
                                            ALU.add).then_inc(y_done, 1)

                def chunk(n):
                    g, c = n // FC, n % FC
                    if c == LAG - 1 and g > 0:
                        residual(g - 1)
                    ve.wait_ge(silu_done, n + 1)
                    ve.wait_ge(u_mm, n + 1)
                    nc.vector.tensor_tensor(gu[:, c % 2, :], s_ps[:, c % 2, :], act[:, c % 2, :],
                                            ALU.mult).then_inc(gu_done, 1)
                    m = PICKS * g + min(c, SHARED)
                    ve.wait_ge(wb_mm, m + 1)
                    ve.wait_ge(gu_done, n + 1)
                    wait(ve, hid_lo_done, n - 1)
                    nc.vector.tensor_tensor(hid[:, n % 2, :], w_bank[m % 2], gu[:, c % 2, :],
                                            ALU.mult).then_inc(hid_done, 1)

                def slot(p, j):
                    def route(place):
                        if on(p - 2):
                            router(p - 2, j, place)

                    if j == 1 and on(p + 1):
                        q = p + 1
                        if at(q, 0):
                            ve.wait_ge(d_x0, 16)
                        if at(q, 1):
                            ve.wait_ge(d_x, 16)
                        for b in range(2):
                            nc.vector.bn_stats(stat1[:, b, :], x_all[:, cols(2 * q + b, 1), :]
                                               .rearrange("p b d -> p (b d)")).then_inc(ln1, 1)
                        wait(ve, ln1, 4 * q + 2)
                        wait(ve, ln1_rstd, 2 * q)
                    split_xt = {7: [(p + 1, 0)], 0: [(p, 1)]}.get(j, [])
                    if at(p, -1):
                        split_xt = [(0, 0), (0, 1)] if j == 6 else []
                    if at(p, 0) and j == 0:
                        split_xt = []
                    for qx, b in split_xt:
                        if not on(qx):
                            continue
                        wait(ve, xt_ready, qx + 1)
                        wait(ve, s_done, UNITS * qx - 1 + b)
                        nc.vector.tensor_copy(xt_hi[:, b, :], xt[:, b * P:(b + 1) * P]).then_inc(xt_split, 1)
                    q, u = shift(p, j, -1)
                    if on(q):
                        wait(ve, exp_done, UNITS * q + u + 1)
                        nc.vector.reciprocal(row_inv[:, u % 2, :], row_sum[:, u % 2, :]).then_inc(inv_done, 1)
                    if at(p, 2) and j == 0:
                        ve.wait_ge(made, 10)
                    route(0)
                    if on(p):
                        wait(ve, s_done, UNITS * p + j + 1)
                        nc.vector.tensor_reduce(neg_max[:, j % 2, :],
                                                s_ps[:, j % 2, :].rearrange("p (h m) -> p h m", h=4),
                                                X, ALU.max, negate=True).then_inc(max_done, 1)
                    for qx, b in split_xt:
                        if not on(qx):
                            continue
                        if at(qx, 0):
                            ve.wait_ge(xt_split, 2 + b)
                        wait(ve, xt_split, 4 * qx + 2 * b + 1)
                        nc.vector.tensor_tensor(xt_lo[:, b, :], xt[:, b * P:(b + 1) * P],
                                                xt_hi[:, b, :].bitcast(F32), ALU.subtract).then_inc(xt_split, 1)
                    if j == 1 and on(p + 1):
                        for b in range(2):
                            nc.vector.bn_aggr(mv1[:, b, :], stat1[:, b, :]).then_inc(ln1, 1)
                    if j == 3 and on(p + 1):
                        q = p + 1
                        wait(ve, ln1_rstd, 2 * q + 2)
                        wait(ve, xt_mm, q)
                        for b in range(2):
                            nc.vector.tensor_scalar(
                                xn[:, b, :], x_all[:, cols(2 * q + b, 1), :].rearrange("p b d -> p (b d)"),
                                mv1[:, b, 0:1], rstd1[:, b:b + 1], ALU.subtract, ALU.mult).then_inc(xn_ready, 1)
                    if j == 4 and on(p - 1):
                        q = p - 1
                        wait(ve, wo_done, UNITS * q + UNITS)
                        wait(ve, xb_ready, q + 1)
                        wait(ve, x1_kept, q)
                        nc.vector.tensor_tensor(x1[:].rearrange("p b d -> p (b d)"), acc_ps[:, 0:2 * P],
                                                xb[:].rearrange("p b d -> p (b d)"), ALU.add).then_inc(x1_done, 1)
                    if j == 5 and on(p - 1):
                        q = p - 1
                        wait(ve, ln2_rstd, 2 * q + 2)
                        for b in range(2):
                            nc.vector.tensor_scalar(x2n[:, b, :], x1[:, b, :], mv2[:, b, 0:1], rstd2[:, b:b + 1],
                                                    ALU.subtract, ALU.mult).then_inc(x2n_ready, 1)
                    route(1)
                    if j == 4 and on(p - 1):
                        q = p - 1
                        wait(ve, x1_done, q + 1)
                        for b in range(2):
                            nc.vector.bn_stats(stat2[:, b, :], x1[:, b, :]).then_inc(ln2, 1)
                        wait(ve, ln2, 4 * q + 2)
                    if chunk_beside(p, j - 1) is not None:
                        chunk(chunk_beside(p, j - 1))
                    q, u = shift(p, j, -2)
                    if on(q) and u % 2 == 0:
                        n = UNITS * q + u
                        wait(ve, t_done, n + 1)
                        wait(ve, av_done, n - 1)
                        nc.vector.tensor_copy(prob_t[:, 0].rearrange("p h t -> p (h t)"),
                                              t_ps[:]).then_inc(pt_done, 1)
                    if j == 4 and on(p - 1):
                        for b in range(2):
                            nc.vector.bn_aggr(mv2[:, b, :], stat2[:, b, :]).then_inc(ln2, 1)
                    route(2)
                    q, z = shift(p, j, 3)
                    if on(q):
                        wait(ve, z_hi_done, UNITS * q + z + 1)
                        zh = z_hi[:, (z // 2) % 2, 2 * (z % 2):2 * (z % 2) + 2].rearrange("p h b m -> p (h b m)")
                        zl = z_lo[:, (z // 2) % 2, 2 * (z % 2):2 * (z % 2) + 2].rearrange("p h b m -> p (h b m)")
                        nc.vector.tensor_tensor(zl, z_ps[:, z % 2, :], zh.bitcast(F32),
                                                ALU.subtract).then_inc(z_lo_done, 1)
                    route(3)
                    if at(p, -1) and j == 1:
                        a_low(0)
                    if at(p, -1) and j == 3:
                        a_low(1)
                    if at(p, -1) and j == 7:
                        a_low(2)
                    if at(p, 0) and j == 1:
                        a_low(3)
                    if (at(p, 0) or at(p, 1)) and j in (2, 4):
                        piece = 2 * p + (2, 4).index(j)
                        ve.wait_ge(d_ctx, 16)
                        split_ctx(2 * P + 4 * P * piece, min(6 * P + 4 * P * piece, T), 2 + 2 * piece)

                for p in (-1, 0, 1):
                    for j in range(UNITS):
                        slot(p, j)
                with ve.Fori(2, PAIRS - 1) as p:
                    for j in range(UNITS):
                        slot(p, j)
                for p in (PAIRS - 1, PAIRS, PAIRS + 1):
                    for j in range(UNITS):
                        slot(p, j)

                for n in range(BESIDE - 1, FC * FG):
                    chunk(n)
                n = FC * FG - 1
                ve.wait_ge(hid_hi_done, n + 1)
                ve.wait_ge(hid_done, n + 1)
                nc.vector.tensor_tensor(hid_lo[:, n % RING, :], hid[:, n % 2, :],
                                        hid_hi[:, n % RING, :].bitcast(F32), ALU.subtract).then_inc(last_low_done, 1)
                residual(FG - 1)

            @block.tensor
            def _(pe):
                mm = nc.tensor.matmul
                def make_a(g):
                    for h in range(4 * g, 4 * g + 4):
                        last = mm(a_bank[g][:, (h % 4) * P:(h % 4) * P + P], wk[:, h * P:(h + 1) * P],
                                  wq[:, h * P:(h + 1) * P], start=True, stop=True)
                    last.then_inc(a_mm, 1)

                pe.wait_ge(d_wk0, 16)
                pe.wait_ge(d_wq0, 16)
                make_a(0)
                make_a(1)

                def split_mm(out, l_hi, l_lo, r_hi, r_lo):
                    mm(out, l_lo, r_hi, start=True, stop=False)
                    mm(out, l_hi, r_lo, start=False, stop=False)
                    return mm(out, l_hi, r_hi, start=False, stop=True)


                def project(n):
                    g, c = n // FC, n % FC
                    if n < FC * FG - 1:
                        pe.wait_ge(hid_lo_done, n + 1)
                    else:
                        pe.wait_ge(last_low_done, 1)
                    if n == 0:
                        pe.wait_ge(w_split, 18)
                        pe.wait_ge(x1_done, PAIRS)
                    if c == 0:
                        wait(pe, y_done, g)
                    unit, k = cols(c, P), n % RING
                    mm(acc_ps[:], wd_lo[:, unit], hid_hi[:, k, :], start=(c == 0), stop=False, skip_group_check=True)
                    mm(acc_ps[:], wd_hi[:, unit], hid_lo[:, k, :], start=False, stop=False, skip_group_check=True)
                    mm(acc_ps[:], wd_hi[:, unit], hid_hi[:, k, :], start=False, stop=(c == FC - 1),
                       skip_group_check=True).then_inc(down_done, 1)

                def chunk(n):
                    g, c = n // FC, n % FC
                    tok = cols(g, TB * P)
                    unit = slice(c * P, (c + 1) * P)
                    if n == 0:
                        pe.wait_ge(w_split, 12)
                        pe.wait_ge(z_lo_done, UNITS * PAIRS)
                        pe.wait_ge(exp_done, UNITS * PAIRS)
                        pe.wait_ge(v_ready, 4 * PAIRS)
                    if n == 1:
                        pe.wait_ge(pt_done, UNITS * PAIRS)
                    if c == 0:
                        pe.wait_ge(x2_split, TB * (g + 1))
                    wait(pe, silu_done, n - 1)
                    split_mm(z_ps[:, c % 2, :], wg_hi[:, unit], wg_lo[:, unit],
                             x2_hi[:, tok], x2_lo[:, tok]).then_inc(g_mm, 1)
                    wait(pe, gu_done, n - 1)
                    split_mm(s_ps[:, c % 2, :], wu_hi[:, unit], wu_lo[:, unit],
                             x2_hi[:, tok], x2_lo[:, tok]).then_inc(u_mm, 1)
                    if c == 0:
                        pe.wait_ge(w3_ready, TB // 2 * (g + 1))
                    if c <= SHARED:
                        m = PICKS * g + c
                        if m >= 2:
                            pe.wait_ge(hid_done, last_of_pick(m - 2) + 1)
                        mm(w_bank[m % 2], pick[:, c, :], w3_all[:, tok], start=True, stop=True).then_inc(wb_mm, 1)
                    if n >= LAG:
                        project(n - LAG)

                def slot(p, j):
                    if chunk_beside(p, j) is not None:
                        chunk(chunk_beside(p, j))
                    if on(p):
                        g, b = j // 2, j % 2
                        wait(pe, z_lo_done, UNITS * p + 2 * g + 2)
                        wait(pe, xt_split, 4 * p + (4 if at(p, 0) else 2 * b + 2))
                        wait(pe, exp_done, UNITS * p + j - 1)
                        split_mm(s_ps[:, j % 2, :].rearrange("p (h m) -> p h m", h=4), xt_hi[:, b, :], xt_lo[:, b, :],
                                 z_hi[:, g % 2, :, b, :], z_lo[:, g % 2, :, b, :]).then_inc(s_done, 1)
                    q, z = shift(p, j, 3)
                    if on(q):
                        if at(q, 0):
                            pe.wait_ge(a_lo_done, 1 + max(z // 2, z % 2))
                            pe.wait_ge(ctx_split, 2)
                        if at(q, 1) and z == 0:
                            pe.wait_ge(ctx_split, 4)
                        if at(q, 2) and z == 0:
                            pe.wait_ge(ctx_split, 10)
                        wait(pe, z_lo_done, UNITS * q + z - 1)
                        for hh in range(2):
                            h = 2 * z + hh
                            last = split_mm(z_ps[:, z % 2, hh * 256:hh * 256 + 256], a_hi[:, h, :], a_lo[:, h, :],
                                            ctx_hi[:, cols(q, 2 * P)], ctx_lo[:, cols(q, 2 * P)])
                        last.then_inc(z_mm, 1)
                    if at(p, -1) and j == 6:
                        pe.wait_ge(d_wk, 16)
                        pe.wait_ge(d_wq, 16)
                        make_a(2)
                    if at(p, 0) and j == 0:
                        make_a(3)
                    q, u = shift(p, j, -2)
                    if on(q):
                        n = UNITS * q + u
                        if at(n, 0):
                            pe.wait_ge(made, 1)
                        wait(pe, norm_done, n + 1)
                        wait(pe, pt_done, n)
                        for h in range(4):
                            last = nc.tensor.transpose(t_ps[:, h * P:(h + 1) * P], prob_n[:, u % 2, h, :], ident[:])
                        last.then_inc(t_done, 1)

                    def o_bank_free():
                        wait(pe, ot_done, many(UNITS * p + j - 3, UNITS * PAIRS))
                        if isinstance(p, int):
                            wait(pe, x1_kept, many(p - 1 - (j <= 1), PAIRS))
                            wait(pe, count_ready, many(p - 1 - (j <= 3), PAIRS))
                            wait(pe, xt_ready, many(p + 2 - (j <= 5), PAIRS))
                            wait(pe, x2t_ready, many(p - (j <= 6), PAIRS))
                            wait(pe, logit_ready, many(p - 1, PAIRS))
                            wait(pe, w3_ready, many(p - 2, PAIRS))

                    if j == 1 and on(p - 2):
                        o_bank_free()
                        wait(pe, x1_done, p - 1)
                        for b in range(2):
                            last = nc.tensor.transpose(aux[:, b * P:(b + 1) * P], x1[:, b, :], ident[:])
                        last.then_inc(x1t_mm, 1)
                    if j == 3 and on(p - 2):
                        o_bank_free()
                        wait(pe, step, WEIGHTS * (p - 2) + CHOICES)
                        mm(aux[:, 0:2 * ED], upto[:], taken[:].rearrange("p b e -> p (b e)"), start=True, stop=False)
                        mm(aux[:, 0:2 * ED], ones[:], carry[:, 0:2, :].rearrange("p b e -> p (b e)"),
                           start=False, stop=True).then_inc(count_mm, 1)
                    if j == 5 and on(p + 1):
                        o_bank_free()
                        if at(p, -1):
                            pe.wait_ge(made, 1)
                        wait(pe, xn_ready, 2 * (p + 1) + 2)
                        for b in range(2):
                            last = nc.tensor.transpose(aux[:, b * P:(b + 1) * P], xn[:, b, :], ident[:])
                        last.then_inc(xt_mm, 1)
                    if j == 6 and on(p - 1):
                        o_bank_free()
                        wait(pe, x2n_ready, 2 * p)
                        for b in range(2):
                            last = nc.tensor.transpose(aux[:, b * P:(b + 1) * P], x2n[:, b, :], ident[:])
                        last.then_inc(x2_mm, 1)
                    if j == 7 and (on(p - 1) or on(p - 2)):
                        o_bank_free()
                    if j == 7 and on(p - 2):
                        wait(pe, step, WEIGHTS * (p - 1))
                        for b in range(2):
                            last = nc.tensor.transpose(aux_b[0:W3K, P + b * P:2 * P + b * P], w3[:, b, :], ident_b[:])
                        last.then_inc(w3_mm, 1)
                    if j == 7 and on(p - 1):
                        if at(p, 1):
                            pe.wait_ge(d_gate, 16)
                        wait(pe, x2t_ready, p)
                        for b in range(2):
                            last = mm(aux[:, b * E:(b + 1) * E], x2t[:, b * P:(b + 1) * P], gate[:],
                                      start=True, stop=True)
                        last.then_inc(logit_mm, 1)
                    q, u = shift(p, j, -3)
                    if on(q):
                        g, b = u // 2, u % 2
                        o_bank_free()
                        wait(pe, pt_done, UNITS * q + u + 1)
                        wait(pe, v_ready, 4 * q + 2 * (g // 2) + b + 1)
                        for h in range(4):
                            half = (h % 2) * DH
                            last = mm(o_ps[half:half + DH, (h // 2) * P:(h // 2) * P + P],
                                      v[:, b, (4 * g + h) * DH:(4 * g + h + 1) * DH], prob_t[:, u % 2, h, :],
                                      start=True, stop=True)
                        last.then_inc(av_done, 1)
                    q, u = shift(p, j, -4)
                    if on(q):
                        g, b = u // 2, u % 2
                        if at(q, 0) and u == 0:
                            pe.wait_ge(d_wo, 16)
                        wait(pe, ot_done, UNITS * q + u + 1)
                        if u == 0:
                            wait(pe, x1_done, q)
                        for c in range(2):
                            last = mm(acc_ps[:, b * P:(b + 1) * P], ot[:, u % 2, c, :], wo[:, 2 * g + c, :],
                                      start=(u == 0 and c == 0), stop=(g == GROUPS - 1 and c == 1),
                                      skip_group_check=True)
                        last.then_inc(wo_done, 1)
                    q, vi = v_chunk(p, j)
                    if on(q):
                        b, half = vi % 2, (vi // 2) * 512
                        if at(p, 0) and j == 0:
                            pe.wait_ge(wv_split, 2)
                        wait(pe, ctxv_ready, 2 * q + 2)
                        wait(pe, v_ready, 4 * q + vi)
                        split_mm(v_ps[:], ctxv_hi[:, b * P:(b + 1) * P], ctxv_lo[:, b * P:(b + 1) * P],
                                 wv_hi[:, half:half + 512], wv_lo[:, half:half + 512]).then_inc(v_mm, 1)

                for p in (-1, 0, 1):
                    for j in range(UNITS):
                        slot(p, j)
                with pe.Fori(2, PAIRS - 1) as p:
                    for j in range(UNITS):
                        slot(p, j)
                for p in (PAIRS - 1, PAIRS, PAIRS + 1):
                    for j in range(UNITS):
                        slot(p, j)

                for n in range(BESIDE, FC * FG):
                    chunk(n)
                for n in range(FC * FG - LAG, FC * FG):
                    project(n)


def kernel(x, ctx_1024, L0_xattn_W_q, L0_xattn_W_k, L0_xattn_W_v, L0_xattn_W_o, L0_xattn_b_o, L0_ffn_gate_w,
           L0_ffn_dyn_gate_w, L0_ffn_dyn_up_w, L0_ffn_dyn_down_w, L0_ffn_sh_gate_w, L0_ffn_sh_up_w,
           L0_ffn_sh_down_w):
    import numpy as np
    import concourse.bacc as bacc
    from concourse.bass_utils import run_bass_kernel_spmd

    def lay(a):
        return np.ascontiguousarray(a)

    x, ctx = np.asarray(x), np.asarray(ctx_1024)
    D = x.shape[-1]
    inner = L0_xattn_W_q.shape[1]
    heads = inner // DH

    def by_head(wt):
        return lay(np.asarray(wt).T.reshape(heads, DH, D).transpose(1, 0, 2).reshape(DH, heads * D))

    def rows(dyn, shared):
        return lay(np.concatenate([np.asarray(dyn).reshape(-1, D), np.asarray(shared).reshape(-1, D)]).T)

    def down(dyn, shared):
        units = np.concatenate([np.asarray(a).transpose(0, 2, 1).reshape(-1, D) for a in (dyn, shared)])
        return lay(units.reshape(-1, P, D).transpose(1, 0, 2).reshape(P, -1))

    arrays = {
        "x_in": lay(x),
        "ctx_t": lay(ctx.reshape(-1, D).T),
        "wq_t": by_head(L0_xattn_W_q),
        "wk_t": by_head(L0_xattn_W_k),
        "w_v": lay(L0_xattn_W_v),
        "w_o": lay(L0_xattn_W_o),
        "b_o": lay(np.asarray(L0_xattn_b_o).reshape(1, D)),
        "gate_t": lay(np.asarray(L0_ffn_gate_w).T),
        "wg_t": rows(L0_ffn_dyn_gate_w, L0_ffn_sh_gate_w),
        "wu_t": rows(L0_ffn_dyn_up_w, L0_ffn_sh_up_w),
        "wd_t": down(L0_ffn_dyn_down_w, L0_ffn_sh_down_w),
    }
    nc = bacc.Bacc("TRN2", target_bir_lowering=False, num_devices=1)
    aps = [nc.dram_tensor(k, a.shape, F32, kind="ExternalInput").ap() for k, a in arrays.items()]
    out_t = nc.dram_tensor("out_t", (D, ctx.shape[0] * ctx.shape[1]), F32, kind="ExternalOutput").ap()
    xattn_moe(nc, *aps, out_t)
    r = run_bass_kernel_spmd(nc, [arrays], core_ids=[0])
    return lay(np.asarray(r.results[0]["out_t"]).T).reshape(x.shape)
```
